# Optimizing a Trainium2 kernel written in Bass

```python
import numpy as np
import jax
import jax.numpy as jnp

def _softmax(x, axis=-1):
    return jax.nn.softmax(x, axis=axis)

def _gelu(x):
    return jax.nn.gelu(x, approximate=True)

def _silu(x):
    return jax.nn.silu(x)

def _sigmoid(x):
    return jax.nn.sigmoid(x)

def _layernorm(x, axis=-1, eps=1e-05):
    m = jnp.mean(x, axis=axis, keepdims=True)
    v = jnp.var(x, axis=axis, keepdims=True)
    return (x - m) / jnp.sqrt(v + eps)

def _scatter_add(tgt, idx, src, axis=0):
    return tgt.at[idx].add(src)

def _segment_sum(src, seg, n):
    return jax.ops.segment_sum(src, seg, n)
kernel_name = 'mk_hybrid_d1_jaxref_r4_ae0862'

def setup_inputs(seed: int=0):
    np.random.seed(seed)
    _w = jnp.asarray

    def _L0_attn_a_setup():
        import jax, jax.numpy as jnp
        import numpy as np
        B, L, D_INNER, D_STATE, DT_RANK = (4, 256, 512, 16, 128)
        key = jax.random.key(seed)
        ks = jax.random.split(key, 4)
        x = jax.random.normal(ks[0], (B, L, D_INNER), dtype=jnp.float32)
        W_x = jax.random.normal(ks[1], (DT_RANK + 2 * D_STATE, D_INNER), dtype=jnp.float32) * 0.02
        W_dt = jax.random.uniform(ks[2], (D_INNER, DT_RANK), dtype=jnp.float32, minval=-0.1, maxval=0.1)
        b_dt = jax.random.normal(ks[3], (D_INNER,), dtype=jnp.float32) * 0.02
        A_log = jnp.log(jnp.tile(jnp.arange(1, D_STATE + 1, dtype=jnp.float32)[None, :], (D_INNER, 1)))
        D_param = jnp.ones((D_INNER,), dtype=jnp.float32)
        return {'x': x, 'W_x': W_x, 'W_dt': W_dt, 'b_dt': b_dt, 'A_log': A_log, 'D_param': D_param}
    _L0_attn_a_in = _L0_attn_a_setup()

    def _L0_attn_b_setup():
        import jax, jax.numpy as jnp
        import numpy as np
        N_EMBD = 512
        Q_HEAD = 16
        KV_HEAD = 4
        HEAD_DIM = N_EMBD // Q_HEAD
        ROPE_BASE = 10000.0

        def _rope(Y, d_rope, base=ROPE_BASE):
            b, h, t, d = Y.shape
            mid = d_rope // 2
            Y1 = Y[:, :mid]
            Y2 = Y[:, mid:]
            Ym1 = jnp.concatenate([Y1, Y2], axis=1)
            Ym2 = jnp.concatenate([-Y2, Y1], axis=1)
            inv = base ** (-2.0 * jnp.arange(d // 2, dtype=jnp.float32) / d)
            theta = jnp.arange(t, dtype=jnp.float32)[:, None] * inv[None, :]
            cos2 = jnp.concatenate([jnp.cos(theta), jnp.cos(theta)], axis=1)
            sin2 = jnp.concatenate([jnp.sin(theta), jnp.sin(theta)], axis=1)
            return Ym1 * cos2 + Ym2 * sin2

        def _attention(x, Wq, bq, Wk, bk, Wv, bv, Wo, bo):
            b, t, n = x.shape
            hd = n // Q_HEAD
            q = x @ Wq.T + bq
            k = x @ Wk.T + bk
            v = x @ Wv.T + bv
            q = q.reshape(b, t, Q_HEAD, hd).transpose(0, 2, 1, 3)
            k = k.reshape(b, t, KV_HEAD, hd).transpose(0, 2, 1, 3)
            v = v.reshape(b, t, KV_HEAD, hd).transpose(0, 2, 1, 3)
            q = _rope(q, N_EMBD)
            k = _rope(k, N_EMBD)
            rep = Q_HEAD // KV_HEAD
            k = jnp.repeat(k, rep, axis=1)
            v = jnp.repeat(v, rep, axis=1)
            scale = jnp.sqrt(jnp.float32(hd))
            att = jnp.einsum('bhqd,bhkd->bhqk', q, k) / scale
            causal = jnp.tril(jnp.ones((t, t), dtype=bool))
            att = jnp.where(causal[None, None], att, -jnp.inf)
            att = jax.nn.softmax(att, axis=-1)
            y = jnp.einsum('bhqt,bhtd->bhqd', att, v)
            y = y.transpose(0, 2, 1, 3).reshape(b, t, n)
            return y @ Wo.T + bo
        key = jax.random.key(seed)
        ks = jax.random.split(key, 9)
        kv_dim = HEAD_DIM * KV_HEAD
        s = 1.0 / np.sqrt(N_EMBD)
        return {'x': jax.random.normal(ks[0], (4, 256, N_EMBD), jnp.float32), 'Wq': jax.random.normal(ks[1], (N_EMBD, N_EMBD), jnp.float32) * s, 'bq': jax.random.normal(ks[2], (N_EMBD,), jnp.float32) * 0.01, 'Wk': jax.random.normal(ks[3], (kv_dim, N_EMBD), jnp.float32) * s, 'bk': jax.random.normal(ks[4], (kv_dim,), jnp.float32) * 0.01, 'Wv': jax.random.normal(ks[5], (kv_dim, N_EMBD), jnp.float32) * s, 'bv': jax.random.normal(ks[6], (kv_dim,), jnp.float32) * 0.01, 'Wo': jax.random.normal(ks[7], (N_EMBD, N_EMBD), jnp.float32) * s, 'bo': jax.random.normal(ks[8], (N_EMBD,), jnp.float32) * 0.01}
    _L0_attn_b_in = _L0_attn_b_setup()

    def _L0_ffn_setup():
        import jax, jax.numpy as jnp
        import numpy as np
        E, K, H, I = (64, 6, 512, 352)
        NS = 2
        IS = NS * I
        CAP = 64
        T_TOKENS = (1, 256)
        SCALE = 0.02

        def _moe_infer(x, gate_w, w_gate, w_up, w_down):
            T = x.shape[0]
            TK = T * K
            logits = x @ gate_w.T
            scores = jax.nn.softmax(logits, axis=-1)
            topk_w, topk_i = jax.lax.top_k(scores, K)
            flat_i = topk_i.reshape(-1)
            flat_w = topk_w.reshape(-1)
            token_ids = jnp.arange(TK, dtype=jnp.int32) // K
            order = jnp.argsort(flat_i)
            sorted_e = flat_i[order]
            counts = jnp.bincount(flat_i, length=E)
            starts = jnp.concatenate([jnp.zeros((1,), counts.dtype), jnp.cumsum(counts)[:-1]])
            pos_sorted = jnp.arange(TK) - starts[sorted_e]
            pos = jnp.zeros((TK,), jnp.int32).at[order].set(pos_sorted.astype(jnp.int32))
            valid = pos < CAP
            slot = jnp.where(valid, pos, CAP)
            buf = jnp.zeros((E, CAP + 1, H), x.dtype).at[flat_i, slot].set(x[token_ids])
            g = jnp.einsum('ech,ehi->eci', buf, w_gate)
            u = jnp.einsum('ech,ehi->eci', buf, w_up)
            y = jnp.einsum('eci,eih->ech', jax.nn.silu(g) * u, w_down)
            out_slots = y[flat_i, slot] * (flat_w * valid)[:, None]
            return out_slots.reshape(T, K, H).sum(axis=1)
        key = jax.random.key(seed)
        ks = jax.random.split(key, 8)
        f32 = jnp.float32
        return {'hidden_states': jax.random.normal(ks[0], (*T_TOKENS, H), f32), 'gate_w': jax.random.normal(ks[1], (E, H), f32) * SCALE, 'w_gate': jax.random.normal(ks[2], (E, H, I), f32) * SCALE, 'w_up': jax.random.normal(ks[3], (E, H, I), f32) * SCALE, 'w_down': jax.random.normal(ks[4], (E, I, H), f32) * SCALE, 'sw_gate': jax.random.normal(ks[5], (H, IS), f32) * SCALE, 'sw_up': jax.random.normal(ks[6], (H, IS), f32) * SCALE, 'sw_down': jax.random.normal(ks[7], (IS, H), f32) * SCALE}
    _L0_ffn_in = _L0_ffn_setup()
    _d = {'L0_attn_a_x': _L0_attn_a_in['x'], 'L0_attn_a_W_x': _L0_attn_a_in['W_x'], 'L0_attn_a_W_dt': _L0_attn_a_in['W_dt'], 'L0_attn_a_b_dt': _L0_attn_a_in['b_dt'], 'L0_attn_a_A_log': _L0_attn_a_in['A_log'], 'L0_attn_a_D_param': _L0_attn_a_in['D_param'], 'L0_attn_b_Wq': _L0_attn_b_in['Wq'], 'L0_attn_b_bq': _L0_attn_b_in['bq'], 'L0_attn_b_Wk': _L0_attn_b_in['Wk'], 'L0_attn_b_bk': _L0_attn_b_in['bk'], 'L0_attn_b_Wv': _L0_attn_b_in['Wv'], 'L0_attn_b_bv': _L0_attn_b_in['bv'], 'L0_attn_b_Wo': _L0_attn_b_in['Wo'], 'L0_attn_b_bo': _L0_attn_b_in['bo'], 'L0_ffn_gate_w': _L0_ffn_in['gate_w'], 'L0_ffn_w_gate': _L0_ffn_in['w_gate'], 'L0_ffn_w_up': _L0_ffn_in['w_up'], 'L0_ffn_w_down': _L0_ffn_in['w_down'], 'L0_ffn_sw_gate': _L0_ffn_in['sw_gate'], 'L0_ffn_sw_up': _L0_ffn_in['sw_up'], 'L0_ffn_sw_down': _L0_ffn_in['sw_down']}
    _x0 = _d['L0_attn_a_x']
    _d['L0_attn_a_x'] = jax.random.normal(jax.random.fold_in(jax.random.key(seed), 1), (8, 512, 512), dtype=_x0.dtype)
    del _x0
    return _d

def reference(L0_attn_a_x, L0_attn_a_W_x, L0_attn_a_W_dt, L0_attn_a_b_dt, L0_attn_a_A_log, L0_attn_a_D_param, L0_attn_b_Wq, L0_attn_b_bq, L0_attn_b_Wk, L0_attn_b_bk, L0_attn_b_Wv, L0_attn_b_bv, L0_attn_b_Wo, L0_attn_b_bo, L0_ffn_gate_w, L0_ffn_w_gate, L0_ffn_w_up, L0_ffn_w_down, L0_ffn_sw_gate, L0_ffn_sw_up, L0_ffn_sw_down):

    def _L0_attn_a_ref(x, W_x, W_dt, b_dt, A_log, D_param):
        import jax, jax.numpy as jnp
        import numpy as np
        B, L, D_INNER, D_STATE, DT_RANK = (4, 256, 512, 16, 128)
        Bn, Ln, Din = x.shape
        xz = jnp.einsum('bld,kd->blk', x, W_x)
        dt_raw = xz[..., :DT_RANK]
        b_ssm = xz[..., DT_RANK:DT_RANK + D_STATE]
        c_ssm = xz[..., DT_RANK + D_STATE:]
        dt = jax.nn.softplus(jnp.einsum('blr,dr->bld', dt_raw, W_dt) + b_dt)
        a = -jnp.exp(A_log)
        d_a = jnp.exp(dt[..., None] * a[None, None])
        dbx = dt[..., None] * b_ssm[:, :, None, :] * x[..., None]

        def step(h, inp):
            da_t, dbx_t, c_t = inp
            h = da_t * h + dbx_t
            y = jnp.einsum('bdn,bn->bd', h, c_t)
            return (h, y)
        h0 = jnp.zeros((Bn, Din, D_STATE), dtype=x.dtype)
        _, ys = jax.lax.scan(step, h0, (jnp.swapaxes(d_a, 0, 1), jnp.swapaxes(dbx, 0, 1), jnp.swapaxes(c_ssm, 0, 1)))
        y = jnp.swapaxes(ys, 0, 1)
        return y + x * D_param

    def _L0_attn_b_ref(x, Wq, bq, Wk, bk, Wv, bv, Wo, bo):
        import jax, jax.numpy as jnp
        import numpy as np
        N_EMBD = 512
        Q_HEAD = 16
        KV_HEAD = 4
        HEAD_DIM = N_EMBD // Q_HEAD
        ROPE_BASE = 10000.0

        def _rope(Y, d_rope, base=ROPE_BASE):
            b, h, t, d = Y.shape
            mid = d_rope // 2
            Y1 = Y[:, :mid]
            Y2 = Y[:, mid:]
            Ym1 = jnp.concatenate([Y1, Y2], axis=1)
            Ym2 = jnp.concatenate([-Y2, Y1], axis=1)
            inv = base ** (-2.0 * jnp.arange(d // 2, dtype=jnp.float32) / d)
            theta = jnp.arange(t, dtype=jnp.float32)[:, None] * inv[None, :]
            cos2 = jnp.concatenate([jnp.cos(theta), jnp.cos(theta)], axis=1)
            sin2 = jnp.concatenate([jnp.sin(theta), jnp.sin(theta)], axis=1)
            return Ym1 * cos2 + Ym2 * sin2

        def _attention(x, Wq, bq, Wk, bk, Wv, bv, Wo, bo):
            b, t, n = x.shape
            hd = n // Q_HEAD
            q = x @ Wq.T + bq
            k = x @ Wk.T + bk
            v = x @ Wv.T + bv
            q = q.reshape(b, t, Q_HEAD, hd).transpose(0, 2, 1, 3)
            k = k.reshape(b, t, KV_HEAD, hd).transpose(0, 2, 1, 3)
            v = v.reshape(b, t, KV_HEAD, hd).transpose(0, 2, 1, 3)
            q = _rope(q, N_EMBD)
            k = _rope(k, N_EMBD)
            rep = Q_HEAD // KV_HEAD
            k = jnp.repeat(k, rep, axis=1)
            v = jnp.repeat(v, rep, axis=1)
            scale = jnp.sqrt(jnp.float32(hd))
            att = jnp.einsum('bhqd,bhkd->bhqk', q, k) / scale
            causal = jnp.tril(jnp.ones((t, t), dtype=bool))
            att = jnp.where(causal[None, None], att, -jnp.inf)
            att = jax.nn.softmax(att, axis=-1)
            y = jnp.einsum('bhqt,bhtd->bhqd', att, v)
            y = y.transpose(0, 2, 1, 3).reshape(b, t, n)
            return y @ Wo.T + bo
        return _attention(x, Wq, bq, Wk, bk, Wv, bv, Wo, bo)

    def _L0_ffn_ref(hidden_states, gate_w, w_gate, w_up, w_down, sw_gate, sw_up, sw_down):
        import jax, jax.numpy as jnp
        import numpy as np
        E, K, H, I = (64, 6, 512, 352)
        NS = 2
        IS = NS * I
        CAP = 64
        T_TOKENS = (1, 256)
        SCALE = 0.02

        def _moe_infer(x, gate_w, w_gate, w_up, w_down):
            T = x.shape[0]
            TK = T * K
            logits = x @ gate_w.T
            scores = jax.nn.softmax(logits, axis=-1)
            topk_w, topk_i = jax.lax.top_k(scores, K)
            flat_i = topk_i.reshape(-1)
            flat_w = topk_w.reshape(-1)
            token_ids = jnp.arange(TK, dtype=jnp.int32) // K
            order = jnp.argsort(flat_i)
            sorted_e = flat_i[order]
            counts = jnp.bincount(flat_i, length=E)
            starts = jnp.concatenate([jnp.zeros((1,), counts.dtype), jnp.cumsum(counts)[:-1]])
            pos_sorted = jnp.arange(TK) - starts[sorted_e]
            pos = jnp.zeros((TK,), jnp.int32).at[order].set(pos_sorted.astype(jnp.int32))
            valid = pos < CAP
            slot = jnp.where(valid, pos, CAP)
            buf = jnp.zeros((E, CAP + 1, H), x.dtype).at[flat_i, slot].set(x[token_ids])
            g = jnp.einsum('ech,ehi->eci', buf, w_gate)
            u = jnp.einsum('ech,ehi->eci', buf, w_up)
            y = jnp.einsum('eci,eih->ech', jax.nn.silu(g) * u, w_down)
            out_slots = y[flat_i, slot] * (flat_w * valid)[:, None]
            return out_slots.reshape(T, K, H).sum(axis=1)
        orig_shape = hidden_states.shape
        x = hidden_states.reshape(-1, orig_shape[-1])
        y = _moe_infer(x, gate_w, w_gate, w_up, w_down).reshape(orig_shape)
        shared = jax.nn.silu(hidden_states @ sw_gate) * (hidden_states @ sw_up) @ sw_down
        return y + shared
    x = L0_attn_a_x
    x = x + _L0_attn_a_ref(_layernorm(x, axis=-1), L0_attn_a_W_x, L0_attn_a_W_dt, L0_attn_a_b_dt, L0_attn_a_A_log, L0_attn_a_D_param)
    x = x + _L0_ffn_ref(_layernorm(x, axis=-1), L0_ffn_gate_w, L0_ffn_w_gate, L0_ffn_w_up, L0_ffn_w_down, L0_ffn_sw_gate, L0_ffn_sw_up, L0_ffn_sw_down)
    x = x + _L0_attn_b_ref(_layernorm(x, axis=-1), L0_attn_b_Wq, L0_attn_b_bq, L0_attn_b_Wk, L0_attn_b_bk, L0_attn_b_Wv, L0_attn_b_bv, L0_attn_b_Wo, L0_attn_b_bo)
    x = x + _L0_ffn_ref(_layernorm(x, axis=-1), L0_ffn_gate_w, L0_ffn_w_gate, L0_ffn_w_up, L0_ffn_w_down, L0_ffn_sw_gate, L0_ffn_sw_up, L0_ffn_sw_down)
    return x

_drawn_inputs = setup_inputs


def setup_inputs(seed=0):
    import zlib

    import numpy as np

    out = dict(_drawn_inputs(seed))
    spreads = {'L0_attn_a_D_param': (1.0, 0.2)}
    factors = {'L0_attn_a_b_dt': 8.0,
     'L0_attn_b_bq': 63.281,
     'L0_attn_b_bk': 62.498,
     'L0_attn_b_bv': 8.0,
     'L0_attn_b_bo': 8.0,
     'L0_ffn_gate_w': 8.0,
     'L0_ffn_w_gate': 8.0,
     'L0_ffn_w_up': 8.0,
     'L0_ffn_w_down': 8.0}
    for name, (base, spread) in spreads.items():
        noise = np.random.default_rng([zlib.crc32(name.encode()), seed]).standard_normal(out[name].shape)
        drawn = base * np.exp(spread * noise) if base else spread * noise
        out[name] = jnp.asarray(drawn.astype(out[name].dtype))
    for name, factor in factors.items():
        out[name] = (out[name] * factor).astype(out[name].dtype)
    return out
```

```python
from contextlib import ExitStack

import numpy as np

import concourse.bass as bass
from concourse import mybir

FP32 = mybir.dt.float32
BF16 = mybir.dt.bfloat16
I32 = mybir.dt.int32
ALU = mybir.AluOpType
ACT = mybir.ActivationFunctionType
AXIS_X = mybir.AxisListType.X

P = 128
BATCH, SEQ, H = 8, 512, 512
T = BATCH * SEQ
NT = T // P
QT = SEQ // P
HC = H // P
NSTATE, DT_RANK = 16, 128
HEADS, KV_HEADS, HEAD = 16, 4, 32
E, TOPK, INTER, CAP = 64, 6, 352, 64
SHARED = 2 * INTER
SLOTS = E * CAP
EPS = 1e-5
NEG = -1e30
BANK = 512
ARENA = 52000


class Lane:

    def __init__(self, nc, name):
        self.nc, self.name, self.queue, self.waited = nc, name, [], {}
        self.sem, self.count, self.sems = None, 0, 0
        self.last, self.mark = None, None

    def new_count(self, ctx):
        self.sem = ctx.enter_context(self.nc.semaphore(f"{self.name}_{self.sems}"))
        self.count, self.sems = 0, self.sems + 1

    def do(self, method, *args, **kw):
        self.last = [method, args, kw, None]
        self.queue.append(self.last)

    def done(self):
        if self.last[3] is None:
            self.count += 1
            self.last[3] = (self.sem, 1)
            self.mark = (self.sem, self.count)
        return self.mark

    def wait(self, *marks):
        for sem, value in marks:
            if self.waited.get(sem.name, 0) < value:
                self.waited[sem.name] = value
                self.queue.append(["wait", sem, value, None])

    def dma(self, method, slot, *args, **kw):
        slot.count += 16
        self.queue.append([method, args, kw, (slot.sem, 16)])
        return (slot.sem, slot.count)

    def play(self, engine):
        for method, args, kw, inc in self.queue:
            if isinstance(method, str):
                engine.wait_ge(args, kw)
            elif inc is None:
                method(*args, **kw)
            else:
                method(*args, **kw).then_inc(*inc)


class Slot:

    def __init__(self, ctx, nc, name):
        self.sem, self.count = ctx.enter_context(nc.semaphore(name)), 0


class Arena:

    def __init__(self, base):
        self.base, self.at = base, 0

    def cut(self, shape, dt=FP32):
        n = int(np.prod(shape))
        words = n if dt in (FP32, I32) else (n + 1) // 2
        words = (words + 7) // 8 * 8
        assert self.at + words <= ARENA, (self.at, words)
        view = self.base[:, self.at:self.at + words]
        self.at += words
        if dt != FP32:
            view = view.bitcast(dt)
        view = view[:, 0:n]
        if len(shape) == 2:
            view = view.rearrange("p (a b) -> p a b", a=shape[0])
        if len(shape) == 3:
            view = view.rearrange("p (a b c) -> p a b c", a=shape[0], b=shape[1])
        return view


def over(ap, axis, n):
    v = ap.unsqueeze(axis)
    shape = list(v.shape)
    shape[axis] = n
    return v.to_broadcast(shape)


class Program:
    def __init__(self, nc, ctx, dram):
        self.nc, self.ctx, self.d = nc, ctx, dram
        base = ctx.enter_context(nc.sbuf_tensor("arena", [P, ARENA], FP32))
        self.sb = Arena(base)
        self.bank = [ctx.enter_context(nc.psum_tensor(f"bank{i}", [P, BANK], FP32)) for i in range(8)]
        self.PE, self.V, self.A, self.G, self.SP = (Lane(nc, n) for n in ("pe", "dve", "act", "pool", "sp"))
        self.lanes = [self.PE, self.V, self.A, self.G, self.SP]
        for lane in self.lanes:
            lane.new_count(ctx)
        self.slots, self.open = {}, []

    def slot(self, name):
        if name not in self.slots:
            self.slots[name] = Slot(self.ctx, self.nc, name)
        return self.slots[name]

    def load(self, name, out, in_):
        mark = self.SP.dma(self.nc.sync.dma_start, self.slot(name), out, in_)
        self.open.append(mark)
        return mark

    store = load

    def stage_end(self):
        marks = [lane.done() for lane in self.lanes[:4] if lane.last]
        last = {}
        for sem, value in self.open:
            last[sem.name] = (sem, max(value, last.get(sem.name, (sem, 0))[1]))
        self.open = []
        for lane in self.lanes:
            lane.wait(*marks, *last.values())
        for lane in self.lanes[:4]:
            lane.new_count(self.ctx)

    def constants(self):
        nc, G, V = self.nc, self.G, self.V
        self.ident = self.sb.cut([P])
        self.half = self.sb.cut([P])
        self.zero = self.sb.cut([H])
        G.do(nc.gpsimd.memset, self.ident, 0.0)
        G.do(nc.gpsimd.memset, self.half, -0.5)
        G.do(nc.gpsimd.memset, self.zero, 0.0)
        G.wait(G.done())
        G.do(nc.gpsimd.affine_select, out=self.ident, in_=self.ident, compare_op=ALU.not_equal, fill=1.0,
             base=0, pattern=[[-1, P]], channel_multiplier=1)
        self.ready = G.done()
        for lane in (self.PE, V, self.A, self.SP, G):
            lane.wait(self.ready)

    def layernorm(self, x, xn, work, x_ready, xn_free=()):
        nc, V, G = self.nc, self.V, self.G
        n = x.shape[1]
        stats, mv, rstd = work
        V.wait(*x_ready)
        for i in range(n):
            V.do(nc.vector.bn_stats, out=stats[:, i, :], in_=x[:, i, :])
        V.wait(V.done())
        for i in range(n):
            V.do(nc.vector.bn_aggr, out=mv[:, i, :], in_=stats[:, i, :])
        G.wait(V.done())
        G.do(nc.gpsimd.tensor_scalar, rstd, mv[:, :, 1], EPS, None, ALU.add)
        G.wait(G.done())
        G.do(nc.gpsimd.tensor_tensor, out=rstd, in0=rstd, in1=self.half[:, 0:n], op=ALU.pow)
        V.wait(G.done(), *xn_free)
        for i in range(n):
            V.do(nc.vector.tensor_scalar, xn[:, i, :], x[:, i, :], mv[:, i, 0:1], rstd[:, i:i + 1],
                 ALU.subtract, ALU.mult)
        return V.done()

    def norm_work(self, n):
        return self.sb.cut([n, 6]), self.sb.cut([n, 2]), self.sb.cut([n])


    def state_space(self, x_dram, out_dram):
        nc, d = self.nc, self.d
        PE, V, A, G, SP = self.lanes
        sb, bank = self.sb, self.bank
        start = sb.at
        NG = 4
        GROUPS = NSTATE // NG
        RING = 3
        wx = sb.cut([HC, DT_RANK + 2 * NSTATE])
        wdt = sb.cut([H])
        par = sb.cut([HC, 2])
        alog = sb.cut([HC, NSTATE])
        xin = [sb.cut([QT, H]) for _ in range(2)]
        xn = sb.cut([QT, H])
        xnT = [sb.cut([HC, SEQ]) for _ in range(2)]
        dt = [sb.cut([HC, SEQ]) for _ in range(2)]
        dtx = [sb.cut([HC, SEQ]) for _ in range(2)]
        soft = sb.cut([HC, SEQ])
        dtr = sb.cut([SEQ])
        bcs = sb.cut([SEQ])
        bb = [sb.cut([NG, SEQ]) for _ in range(RING)]
        cb = [sb.cut([NG, SEQ]) for _ in range(RING)]
        da = [sb.cut([NG, SEQ]) for _ in range(2)]
        hb = [sb.cut([NG, SEQ]) for _ in range(3)]
        yT = xn
        xo = soft
        work = self.norm_work(QT)
        x_v = x_dram.rearrange("(n p) h -> p n h", p=P)
        o_v = out_dram.rearrange("(n p) h -> p n h", p=P)
        bc_dram = d["bc"]

        w_in = [self.load("ss_w", wx, d["wxT"].rearrange("(c p) k -> p c k", p=P)),
                self.load("ss_w", wdt, d["wdtT"]),
                self.load("ss_w", par, d["par"]),
                self.load("ss_w", alog, d["A_log"].rearrange("(c p) n -> p c n", p=P))][-1:]
        for lane in (PE, V, A, G):
            lane.wait(*w_in)
        A.do(nc.scalar.activation, alog, alog, ACT.Exp)
        V.wait(A.done())
        V.do(nc.vector.tensor_scalar, alog, alog, -1.0, None, ALU.mult)
        for t in da:
            V.do(nc.vector.memset, t[:, :, 0:1], 0.0)
        A.wait(V.done())

        xload, prepared, bcload = {}, {}, {}
        bank_free, nbank = [()] * 8, [0]

        def spare():
            i = 4 + nbank[0] % 4
            nbank[0] += 1
            PE.wait(*bank_free[i])
            return i

        xin_free, xnT_free, dt_free = [(), ()], [(), ()], [(), ()]
        ring_free = [()] * RING
        y_free = [()] * HC
        st = {"soft": (), "dtr": (), "bcs": (), "xn": ()}

        def load_x(b):
            SP.wait(*xin_free[b % 2])
            xload[b] = self.load(f"ss_x{b % 2}", xin[b % 2], x_v[:, b * QT:(b + 1) * QT, :])

        def prepare(b):
            s = b % 2
            normed = self.layernorm(xin[s], xn, work, [xload[b]], st["xn"])
            PE.wait(normed)
            A.wait(*xnT_free[s])
            for c in range(HC):
                i = spare()
                for t in range(QT):
                    PE.do(nc.tensor.transpose, bank[i][:, t * P:(t + 1) * P], xn[:, t, c * P:(c + 1) * P],
                          self.ident)
                A.wait(PE.done())
                A.do(nc.scalar.copy, xnT[s][:, c, :], bank[i][:, :])
                bank_free[i] = (A.done(),)
            st["xn"] = (PE.done(),)
            turned = A.done()
            PE.wait(turned)
            i = spare()
            for c in range(HC):
                PE.do(nc.tensor.matmul, bank[i][:, :], wx[:, c, 0:DT_RANK], xnT[s][:, c, :],
                      start=c == 0, stop=c == HC - 1)
            A.wait(PE.done(), *st["dtr"])
            A.do(nc.scalar.copy, dtr, bank[i][:, :])
            bank_free[i] = (A.done(),)
            PE.wait(A.done())
            i = spare()
            R = 2 * NSTATE
            for c in range(HC):
                PE.do(nc.tensor.matmul, bank[i][0:R, :], wx[:, c, DT_RANK:], xnT[s][:, c, :],
                      start=c == 0, stop=c == HC - 1)
            A.wait(PE.done(), *st["bcs"])
            A.do(nc.scalar.copy, bcs[0:R, :], bank[i][0:R, :])
            bank_free[i] = (A.done(),)
            SP.wait(A.done())
            stored = self.store("ss_bc", bc_dram[b, :, :], bcs[0:R, :])
            st["bcs"] = (stored,)
            prepared[b] = [stored]
            A.wait(*dt_free[s], *st["soft"])
            for c in range(HC):
                i = spare()
                PE.do(nc.tensor.matmul, bank[i][:, :], wdt[:, c * P:(c + 1) * P], dtr, start=True, stop=True)
                A.wait(PE.done())
                A.do(nc.scalar.activation, soft[:, c, :], bank[i][:, :], ACT.Abs, bias=par[:, c, 0:1])
                A.do(nc.scalar.activation, dt[s][:, c, :], bank[i][:, :], ACT.Relu, bias=par[:, c, 0:1])
                bank_free[i] = (A.done(),)
            st["dtr"] = (PE.done(),)
            A.wait(A.done())
            A.do(nc.scalar.activation, soft, soft, ACT.Exp, scale=-1.0)
            A.wait(A.done())
            A.do(nc.scalar.activation, soft, soft, ACT.Ln, bias=1.0)
            G.wait(A.done())
            G.do(nc.gpsimd.tensor_tensor, out=dt[s], in0=dt[s], in1=soft, op=ALU.add)
            G.wait(G.done())
            st["soft"] = (G.done(),)
            G.do(nc.gpsimd.tensor_tensor, out=dtx[s], in0=dt[s], in1=xnT[s], op=ALU.mult)
            prepared[b].append(G.done())

        def load_bc(b, g):
            r = (b * GROUPS + g) % RING
            SP.wait(prepared[b][0], *ring_free[r])
            for buf, row, name in ((bb, 0, "b"), (cb, NSTATE, "c")):
                src = bc_dram[b, row + g * NG:row + (g + 1) * NG, :].partition_broadcast(P)
                bcload[b, g, name] = self.load(f"ss_{name}{r}", buf[r], src)

        load_x(0)
        prepare(0)
        load_x(1)
        for g in range(RING):
            load_bc(0, g)
        steps = [(b, g, c) for b in range(BATCH) for g in range(GROUPS) for c in range(HC)]
        scanned, summed, multiplied = {}, {}, {}
        for k in range(len(steps) + 1):
            if k < len(steps):
                b, g, c = steps[k]
                s, r = b % 2, (b * GROUPS + g) % RING
                if k == 0 or c == 0:
                    A.wait(prepared[b][1])
                    G.wait(prepared[b][1])
                if k >= 2:
                    A.wait(scanned[k - 2])
                for n in range(NG):
                    A.do(nc.scalar.activation, da[k % 2][:, n, 1:SEQ], dt[s][:, c, 1:SEQ], ACT.Exp,
                         scale=alog[:, c, g * NG + n:g * NG + n + 1])
                decay = A.done()
                G.wait(bcload[b, g, "b"])
                if k >= 3:
                    G.wait(summed[k - 3])
                G.do(nc.gpsimd.tensor_tensor, out=hb[k % 3], in0=over(dtx[s][:, c, :], 1, NG), in1=bb[r],
                     op=ALU.mult)
                inflow = G.done()
                V.wait(decay, inflow)
                flat = "p a b -> p (a b)"
                V.do(nc.vector.tensor_tensor_scan, out=hb[k % 3].rearrange(flat), data0=da[k % 2].rearrange(flat),
                     data1=hb[k % 3].rearrange(flat), initial=0.0, op0=ALU.mult, op1=ALU.add)
                scanned[k] = V.done()
            if k >= 1:
                b, g, c = steps[k - 1]
                r = (b * GROUPS + g) % RING
                V.wait(scanned[k - 1], bcload[b, g, "c"])
                w = hb[(k - 1) % 3]
                V.do(nc.vector.tensor_tensor, out=w, in0=w, in1=cb[r], op=ALU.mult)
                multiplied[k - 1] = V.done()
                PE.wait(multiplied[k - 1])
                if g == 0:
                    PE.wait(*y_free[c])
                for n in range(NG):
                    PE.do(nc.tensor.matmul, bank[c][:, :], self.ident, w[:, n, :],
                          start=g == 0 and n == 0, stop=g == GROUPS - 1 and n == NG - 1)
                summed[k - 1] = PE.done()
                if c == HC - 1:
                    ring_free[r] = (V.done(), G.done())
                    nb, ng = divmod(b * GROUPS + g + RING, GROUPS)
                    if nb < BATCH and nb in prepared:
                        load_bc(nb, ng)
                    if g == 0 and b + 1 < BATCH:
                        prepare(b + 1)
                        if b * GROUPS + g + RING >= (b + 1) * GROUPS:
                            load_bc(b + 1, 0)
                if g == GROUPS - 1 and c == HC - 1:
                    s = b % 2
                    V.wait(summed[k - 1], *st["xn"], *st.get("yT", ()))
                    for cc in range(HC):
                        V.do(nc.vector.scalar_tensor_tensor, out=yT[:, cc, :], in0=xnT[s][:, cc, :],
                             scalar=par[:, cc, 1:2], in1=bank[cc][:, :], op0=ALU.mult, op1=ALU.add)
                        y_free[cc] = (V.done(),)
                    xnT_free[s] = (V.done(), G.done(), PE.done())
                    dt_free[s] = (A.done(), G.done())
                    PE.wait(V.done())
                    for t in range(QT):
                        i = spare()
                        for cc in range(HC):
                            PE.do(nc.tensor.transpose, bank[i][:, cc * P:(cc + 1) * P],
                                  yT[:, cc, t * P:(t + 1) * P], self.ident)
                        V.wait(PE.done(), *st["soft"], *st.get("xo", ()))
                        V.do(nc.vector.tensor_tensor, out=xo[:, t, :], in0=xin[s][:, t, :], in1=bank[i][:, :],
                             op=ALU.add)
                        bank_free[i] = (V.done(),)
                    st["xn"] = (PE.done(),)
                    xin_free[s] = (V.done(),)
                    SP.wait(V.done())
                    stored = self.store("ss_out", o_v[:, b * QT:(b + 1) * QT, :], xo)
                    st["xo"] = (stored,)
                    st["soft"] = (stored,)
                    if b + 2 < BATCH:
                        load_x(b + 2)
        self.stage_end()
        sb.at = start


    def feed_forward(self, x_dram, a_dram, y_dram):
        nc, d = self.nc, self.d
        PE, V, A, G, SP = self.lanes
        sb, bank = self.sb, self.bank
        start = sb.at
        xn_dram, tab = d["xn"], d["tab"]
        x_v = x_dram.rearrange("(n p) h -> p n h", p=P)
        n_v = xn_dram[0:T, :].rearrange("(n p) h -> p n h", p=P)
        y_v = y_dram[0:T, :].rearrange("(n p) h -> p n h", p=P)

        xnT = sb.cut([HC, T])
        ids = sb.cut([E], I32)
        wts = sb.cut([E])
        region = sb.at

        gw = sb.cut([HC, E])
        tri = sb.cut([P], BF16)
        ones = sb.cut([P], BF16)
        trif = sb.cut([P])
        token = sb.cut([NT])
        first = sb.cut([E])
        pad = sb.cut([E, 2])
        xt = [sb.cut([1, H]) for _ in range(3)]
        xn = [sb.cut([1, H]) for _ in range(2)]
        work = self.norm_work(1)
        NB = 2
        score = [sb.cut([E + 2]) for _ in range(NB)]
        marked = sb.cut([E + 2])
        mask = [sb.cut([E], BF16) for _ in range(NB)]
        seen = [sb.cut([E], BF16) for _ in range(2)]
        small = sb.cut([8])
        top = sb.cut([8])
        six = sb.cut([8])
        valid = sb.cut([E])
        code = [sb.cut([E]) for _ in range(NB)]
        best = sb.cut([8])
        where = [sb.cut([8], I32) for _ in range(NB)]
        equal = sb.cut([TOPK, E])
        pair = [sb.cut([TOPK, 2]) for _ in range(NB)]
        tabin = sb.cut([E, 2])

        w_in = self.load("ff_w", gw, d["gate_wT"].rearrange("(p c) e -> p c e", c=HC))
        G.do(nc.gpsimd.memset, trif, 1.0)
        G.do(nc.gpsimd.memset, ones, 1.0)
        G.do(nc.gpsimd.memset, seen[0], 0.0)
        G.do(nc.gpsimd.memset, six, -1.0)
        for s in score:
            G.do(nc.gpsimd.memset, s[:, E:E + 2], -1.0)
        G.do(nc.gpsimd.memset, pad, 0.0)
        G.do(nc.gpsimd.iota, token, pattern=[[P, NT]], base=0, channel_multiplier=1,
             allow_small_or_imprecise_dtypes=True)
        G.do(nc.gpsimd.iota, first, pattern=[[-CAP, E]], base=SLOTS, channel_multiplier=0,
             allow_small_or_imprecise_dtypes=True)
        G.wait(G.done())
        G.do(nc.gpsimd.affine_select, out=trif, in_=trif, compare_op=ALU.is_gt, fill=0.0, base=0,
             pattern=[[1, P]], channel_multiplier=-1)
        G.do(nc.gpsimd.iota, pad[:, :, 0], pattern=[[0, E]], base=T, channel_multiplier=1,
             allow_small_or_imprecise_dtypes=True)
        G.wait(G.done())
        G.do(nc.gpsimd.tensor_copy, tri, trif)
        set_up = G.done()
        for lane in (PE, V, SP):
            lane.wait(set_up)
        PE.wait(w_in)
        padded = self.store("ff_pad", tab.rearrange("(e c) t -> c e t", c=CAP), pad[0:CAP])
        self.store("ff_pad2", xn_dram[T:T + CAP, :], self.zero[0:CAP, :])
        for b in range(NT):
            self.store("ff_zero", y_v[:, b, :], self.zero)
        self.store("ff_zero", y_dram[T:T + CAP, :], self.zero[0:CAP, :])

        x_free, xn_free, xload = [(), (), ()], [(), ()], {}
        bank_free = [()] * 8
        where_free, score_free = [()] * NB, [()] * NB

        def load_x(i):
            SP.wait(*x_free[i % 3])
            xload[i] = self.load(f"ff_x{i % 3}", xt[i % 3][:, 0, :], x_v[:, i, :])

        load_x(0)
        load_x(1)
        for i in range(NT):
            if i + 2 < NT:
                load_x(i + 2)
            s, tb = i % NB, i % 2
            normed = self.layernorm(xt[i % 3], xn[i % 2], work, [xload[i]], xn_free[i % 2])
            x_free[i % 3] = (normed,)
            SP.wait(normed)
            stored = self.store(f"ff_n{i % 2}", n_v[:, i, :], xn[i % 2][:, 0, :])
            PE.wait(normed, *bank_free[tb])
            cols = xn[i % 2][:, 0, :].rearrange("p (m c) -> p c m", c=HC)
            for c in range(HC):
                PE.do(nc.tensor.transpose, bank[tb][:, c * P:(c + 1) * P], cols[:, c, :], self.ident)
            xn_free[i % 2] = (PE.done(), stored)
            A.wait(PE.done())
            A.do(nc.scalar.copy, xnT[:, :, i * P:(i + 1) * P],
                 bank[tb][:, :].rearrange("p (c t) -> p c t", c=HC))
            bank_free[tb] = (A.done(),)
            PE.wait(A.done(), *bank_free[2 + tb])
            logits = bank[2 + tb][:, 0:E]
            for c in range(HC):
                PE.do(nc.tensor.matmul, logits, xnT[:, c, i * P:(i + 1) * P], gw[:, c, :],
                      start=c == 0, stop=c == HC - 1)
            V.wait(PE.done())
            V.do(nc.vector.tensor_reduce, out=small[:, 0:1], in_=logits, axis=AXIS_X, op=ALU.max, negate=True)
            A.wait(V.done(), *score_free[s])
            A.do(nc.scalar.activation, score[s][:, 0:E], logits, ACT.Exp, bias=small[:, 0:1],
                 accum_out=small[:, 1:2])
            bank_free[2 + tb] = (A.done(),)
            V.wait(A.done())
            V.do(nc.vector.reciprocal, small[:, 2:3], small[:, 1:2])
            V.wait(V.done())
            V.do(nc.vector.tensor_scalar, score[s][:, 0:E], score[s][:, 0:E], small[:, 2:3], None, ALU.mult)
            V.wait(V.done())
            V.do(nc.vector.max, out=top, in_=score[s][:, 0:E])
            V.wait(V.done())
            V.do(nc.vector.tensor_copy, six[:, 0:TOPK], top[:, 0:TOPK])
            V.wait(V.done())
            V.do(nc.vector.match_replace, out=marked, in_to_replace=six, in_values=score[s], imm_value=-2.0)
            V.wait(V.done())
            if i >= NB:
                V.wait(*bank_free[4 + tb])
            V.do(nc.vector.tensor_scalar, mask[s], marked[:, 0:E], -2.0, None, ALU.is_equal)
            masked = V.done()
            PE.wait(masked, *bank_free[4 + tb])
            pos = bank[4 + tb][:, 0:E]
            PE.do(nc.tensor.matmul, pos, tri, mask[s], start=True, stop=False)
            PE.do(nc.tensor.matmul, pos, ones, seen[i % 2], start=False, stop=True)
            counted = PE.done()
            V.wait(masked, counted)
            V.do(nc.vector.tensor_tensor, out=seen[(i + 1) % 2], in0=seen[i % 2], in1=mask[s], op=ALU.add)
            V.do(nc.vector.scalar_tensor_tensor, out=valid, in0=pos, scalar=float(CAP), in1=mask[s],
                 op0=ALU.is_lt, op1=ALU.mult)
            V.do(nc.vector.scalar_tensor_tensor, out=code[s], in0=pos, scalar=-1.0, in1=first,
                 op0=ALU.mult, op1=ALU.add)
            bank_free[4 + tb] = (V.done(),)
            V.wait(V.done())
            V.do(nc.vector.tensor_tensor, out=code[s], in0=code[s], in1=valid, op=ALU.mult)
            V.wait(V.done())
            V.do(nc.vector.max, out=best, in_=code[s])
            V.wait(V.done(), *where_free[s])
            V.do(nc.vector.tensor_scalar, where[s], best, -1.0, float(SLOTS), ALU.mult, ALU.add)
            V.do(nc.vector.tensor_tensor, out=equal, in0=over(code[s], 1, TOPK),
                 in1=over(best[:, 0:TOPK], 2, E), op=ALU.is_equal)
            V.wait(V.done())
            V.do(nc.vector.tensor_tensor, out=equal, in0=equal, in1=over(score[s][:, 0:E], 1, TOPK),
                 op=ALU.mult)
            V.wait(V.done())
            V.do(nc.vector.tensor_reduce, out=pair[s][:, :, 1], in_=equal, axis=AXIS_X, op=ALU.add)
            V.do(nc.vector.tensor_copy, pair[s][:, :, 0], token[:, i:i + 1].to_broadcast([P, TOPK]))
            score_free[s] = (V.done(),)
            G.wait(V.done(), padded)
            for k in range(TOPK):
                mark = G.dma(nc.gpsimd.indirect_dma_start, self.slot(f"ff_s{s}"), out=tab[:, :],
                             out_offset=bass.IndirectOffsetOnAxis(ap=where[s][:, k:k + 1], axis=0),
                             in_=pair[s][:, k, :], in_offset=None, bounds_check=SLOTS - 1, oob_is_err=False)
            self.open.append(mark)
            where_free[s] = (mark,)
        self.stage_end()
        read = self.load("ff_tab", tabin[0:CAP], tab.rearrange("(e c) t -> c e t", c=CAP))
        V.wait(read)
        V.do(nc.vector.tensor_copy, ids[0:CAP, :], tabin[0:CAP, :, 0])
        V.do(nc.vector.tensor_copy, wts[0:CAP, :], tabin[0:CAP, :, 1])
        self.stage_end()

        sb.at = region
        IC = 3
        last = INTER - 2 * P
        WR, XR = 3, 3
        wg = [sb.cut([HC, INTER]) for _ in range(WR)]
        wu = [sb.cut([HC, INTER]) for _ in range(WR)]
        wd = [sb.cut([IC, H]) for _ in range(WR)]
        xe = [sb.cut([H]) for _ in range(XR)]
        xeT = [sb.cut([HC, CAP]) for _ in range(2)]
        sg = [sb.cut([IC, CAP]) for _ in range(2)]
        hT = [sb.cut([IC, CAP]) for _ in range(2)]
        ye = [sb.cut([H]) for _ in range(2)]
        SC = (SHARED + P - 1) // P
        swg, swu = sb.cut([HC, SHARED]), sb.cut([HC, SHARED])
        swd = sb.cut([SC, H])
        shT = sb.cut([SC, BANK])
        ssg = [sb.cut([BANK]) for _ in range(2)]
        xr = [sb.cut([H]) for _ in range(2)]
        yo = [sb.cut([H]) for _ in range(2)]
        last_s = SHARED - (SC - 1) * P
        self.load("ff_sw", swg, d["sw_gate"].rearrange("(p c) i -> p c i", c=HC))
        self.load("ff_sw", swu, d["sw_up"].rearrange("(p c) i -> p c i", c=HC))
        self.load("ff_sw", swd[:, 0:SC - 1, :], d["sw_down"][0:(SC - 1) * P, :].rearrange("(j p) h -> p j h", p=P))
        sw_in = self.load("ff_sw", swd[0:last_s, SC - 1, :], d["sw_down"][(SC - 1) * P:, :])
        for i in (1, 2):
            V.do(nc.vector.memset, bank[i][last:P, :], 0.0)
        cleared = V.done()
        PE.wait(cleared)

        wload, xload, w_free, xe_free = {}, {}, [()] * WR, [()] * XR
        xeT_free, sg_free, hT_free, ye_free, g_free = [()] * 2, [()] * 2, [()] * 2, [()] * 2, [()] * 2
        o = {"t": (), "y": (), "sum": ()}
        turned = {}

        def load_w(e):
            r = e % WR
            SP.wait(*w_free[r])
            self.load(f"ff_w{r}", wg[r], d["w_gate"][e].rearrange("(p c) i -> p c i", c=HC))
            self.load(f"ff_w{r}", wu[r], d["w_up"][e].rearrange("(p c) i -> p c i", c=HC))
            self.load(f"ff_w{r}", wd[r][:, 0:2, :], d["w_down"][e, 0:2 * P, :].rearrange("(j p) h -> p j h", p=P))
            wload[e] = self.load(f"ff_w{r}", wd[r][0:last, 2, :], d["w_down"][e, 2 * P:, :])

        def gather(e):
            r = e % XR
            G.wait(*xe_free[r])
            xload[e] = G.dma(nc.gpsimd.indirect_dma_start, self.slot(f"ff_xe{r}"), out=xe[r][0:CAP, :],
                             out_offset=None, in_=xn_dram[:, :],
                             in_offset=bass.IndirectOffsetOnAxis(ap=ids[0:CAP, e:e + 1], axis=0),
                             bounds_check=T + CAP - 1, oob_is_err=True)
            self.open.append(xload[e])

        def turn(e):
            PE.wait(xload[e], *o["t"])
            cols = xe[e % XR][0:CAP, :].rearrange("p (m c) -> p c m", c=HC)
            for c in range(HC):
                PE.do(nc.tensor.transpose, bank[0][:, c * CAP:(c + 1) * CAP], cols[:, c, :],
                      self.ident[0:CAP, 0:CAP])
            xe_free[e % XR] = (PE.done(),)
            V.wait(PE.done(), *xeT_free[e % 2])
            V.do(nc.vector.tensor_copy, xeT[e % 2], bank[0][:, 0:HC * CAP].rearrange("p (c t) -> p c t", c=HC))
            turned[e] = V.done()
            o["t"] = (V.done(),)

        def up(e):
            r, s = e % WR, e % 2
            PE.wait(wload[e], turned[e], *g_free[s])
            gu = bank[1 + s][:, 0:2 * IC * CAP].rearrange("p (w j t) -> p w j t", w=2, j=IC)
            for w, wt in ((0, wg), (1, wu)):
                for j in range(IC):
                    m = P if j < 2 else last
                    for c in range(HC):
                        PE.do(nc.tensor.matmul, gu[0:m, w, j, :], wt[r][:, c, j * P:j * P + m],
                              xeT[s][:, c, :], start=c == 0, stop=c == HC - 1)
            xeT_free[s] = (PE.done(),)
            A.wait(PE.done(), *sg_free[s])
            A.do(nc.scalar.activation, sg[s], gu[:, 0], ACT.Silu)
            V.wait(A.done(), PE.done(), *hT_free[s])
            V.do(nc.vector.tensor_tensor, out=hT[s], in0=sg[s], in1=gu[:, 1], op=ALU.mult)
            g_free[s] = sg_free[s] = (V.done(),)
            return V.done()

        def down(e, hidden):
            r, s = e % WR, e % 2
            PE.wait(hidden, *o["y"])
            for j in range(IC):
                m = P if j < 2 else last
                PE.do(nc.tensor.matmul, bank[3][0:CAP, :], hT[s][0:m, j, :], wd[r][0:m, j, :],
                      start=j == 0, stop=j == IC - 1)
            w_free[r] = hT_free[s] = (PE.done(),)
            A.wait(PE.done(), *ye_free[s])
            A.do(nc.scalar.activation, ye[s][0:CAP, :], bank[3][0:CAP, :], ACT.Copy, scale=wts[0:CAP, e:e + 1])
            o["y"] = (A.done(),)
            G.wait(A.done(), *o["sum"])
            mark = G.dma(nc.gpsimd.indirect_dma_start, self.slot("ff_sum"), out=y_dram[:, :],
                         out_offset=bass.IndirectOffsetOnAxis(ap=ids[0:CAP, e:e + 1], axis=0),
                         in_=ye[s][0:CAP, :], in_offset=None, bounds_check=T + CAP - 1, oob_is_err=True,
                         compute_op=ALU.add)
            self.open.append(mark)
            ye_free[s] = (mark,)
            o["sum"] = (mark,)

        sh = {"ssg": [(), ()], "h": [], "xr": {}, "xr_free": [(), ()], "yo_free": [(), ()],
              "b4": (), "b5": (), "h_free": (), "ob": [(), ()]}

        def shared_up(q, j):
            m = P if j < SC - 1 else last_s
            toks = slice(q * BANK, (q + 1) * BANK)
            PE.wait(sw_in, *sh["b4"])
            for w, bk in ((swg, 4), (swu, 5)):
                for c in range(HC):
                    PE.do(nc.tensor.matmul, bank[bk][0:m, :], w[:, c, j * P:j * P + m], xnT[:, c, toks],
                          start=c == 0, stop=c == HC - 1)
            A.wait(PE.done(), *sh["ssg"][j % 2])
            A.do(nc.scalar.activation, ssg[j % 2][0:m, :], bank[4][0:m, :], ACT.Silu)
            V.wait(A.done(), PE.done(), *sh["h_free"])
            V.do(nc.vector.tensor_tensor, out=shT[0:m, j, :], in0=ssg[j % 2][0:m, :], in1=bank[5][0:m, :],
                 op=ALU.mult)
            sh["ssg"][j % 2] = (V.done(),)
            sh["b4"] = (V.done(),)
            sh["h"] = (V.done(),)

        def shared_down(q, t):
            i = q * (BANK // P) + t
            s = i % 2
            SP.wait(*sh["xr_free"][s])
            got = self.load(f"ff_xr{s}", xr[s], x_v[:, i, :])
            PE.wait(*sh["h"], *sh["ob"][s])
            for j in range(SC):
                m = P if j < SC - 1 else last_s
                PE.do(nc.tensor.matmul, bank[6 + s][:, :], shT[0:m, j, t * P:(t + 1) * P], swd[0:m, j, :],
                      start=j == 0, stop=j == SC - 1)
            if t == BANK // P - 1:
                sh["h_free"] = (PE.done(),)
            V.wait(PE.done(), got, *sh["yo_free"][s])
            V.do(nc.vector.tensor_tensor, out=yo[s], in0=xr[s], in1=bank[6 + s][:, :], op=ALU.add)
            sh["ob"][s] = sh["xr_free"][s] = (V.done(),)
            SP.wait(V.done())
            sh["yo_free"][s] = (self.store(f"ff_yo{s}", a_dram[i * P:(i + 1) * P, :], yo[s]),)

        units = []
        for q in range(T // BANK):
            units += [(shared_up, q, j) for j in range(SC)] + [(shared_down, q, t) for t in range(BANK // P)]
        spent = 0
        for e in range(WR - 1):
            load_w(e)
        gather(0)
        gather(1)
        turn(0)
        for e in range(E):
            if e + WR - 1 < E:
                load_w(e + WR - 1)
            if e + 2 < E:
                gather(e + 2)
            hidden = up(e)
            if e + 1 < E:
                turn(e + 1)
            upto = (e + 1) * len(units) // E
            for f, q, j in units[spent:upto]:
                f(q, j)
            spent = upto
            down(e, hidden)
        self.stage_end()
        sb.at = start


    def attention(self, a_dram, y_dram, out_dram):
        nc, d = self.nc, self.d
        PE, V, A, G, SP = self.lanes
        sb, bank = self.sb, self.bank
        start = sb.at
        SCALE = float(1.0 / np.sqrt(np.float32(HEAD)))
        KV = KV_HEADS * HEAD
        wq, wk, wv = sb.cut([HC, H]), sb.cut([HC, KV]), sb.cut([HC, KV])
        wo = sb.cut([HC, H])
        bq, bk = sb.cut([HC]), sb.cut([1])
        bv, bo = sb.cut([KV]), sb.cut([H])
        rope = sb.cut([SEQ])
        mask = sb.cut([SEQ])
        xa = [sb.cut([QT, H]) for _ in range(2)]
        xy = [sb.cut([QT, H]) for _ in range(2)]
        xn = sb.cut([QT, H])
        xnT = sb.cut([HC, SEQ])
        qT = [sb.cut([HC, SEQ]) for _ in range(2)]
        kT = [sb.cut([SEQ]) for _ in range(2)]
        vv = [sb.cut([QT, KV]) for _ in range(2)]
        NS, NP = 3, 3
        sc = [sb.cut([SEQ]) for _ in range(NS)]
        pr = [sb.cut([SEQ]) for _ in range(NP)]
        prT = [sb.cut([SEQ]) for _ in range(2)]
        nb = sb.cut([2 * HEADS])
        den = [sb.cut([HEADS]) for _ in range(2)]
        rden = sb.cut([HEADS])
        yn = [sb.cut([HEADS, HEAD]) for _ in range(2)]
        ynT = sb.cut([HC, P])
        xo = [sb.cut([H]) for _ in range(2)]
        work = self.norm_work(QT)

        for out, in_ in ((wq, d["wqT"].rearrange("(c p) n -> p c n", p=P)),
                         (wk, d["wkT"].rearrange("(c p) n -> p c n", p=P)),
                         (wv, d["wvT"].rearrange("(c p) n -> p c n", p=P)),
                         (wo, d["woT"].rearrange("(c p) n -> p c n", p=P)),
                         (bq, d["bq"]),
                         (bk, d["bk"]),
                         (bv, d["bv"].partition_broadcast(P)),
                         (bo, d["bo"].partition_broadcast(P)),
                         (rope, d["rope"])):
            w_in = self.load("at_w", out, in_)
        G.do(nc.gpsimd.memset, mask, 0.0)
        G.wait(G.done())
        G.do(nc.gpsimd.affine_select, out=mask[:, SEQ - P:], in_=mask[:, SEQ - P:], compare_op=ALU.is_ge,
             fill=NEG, base=0, pattern=[[-1, P]], channel_multiplier=1)
        for lane in (PE, V, A):
            lane.wait(w_in, G.done())

        a_v = a_dram.rearrange("(n p) h -> p n h", p=P)
        y_v = y_dram[0:T, :].rearrange("(n p) h -> p n h", p=P)
        o_v = out_dram.rearrange("(n p) h -> p n h", p=P)
        got, xa_free, xy_free, proj_free = {}, [(), ()], [(), ()], [(), ()]
        bank_free = [()] * 8
        st = {"xn": (), "xnT": (), "pj": 0}
        ready = {}

        def load_x(b):
            s = b % 2
            SP.wait(*xa_free[s], *xy_free[s])
            self.load(f"at_a{s}", xa[s], a_v[:, b * QT:(b + 1) * QT, :])
            got[b] = [self.load(f"at_y{s}", xy[s], y_v[:, b * QT:(b + 1) * QT, :]), (self.slot(f"at_a{s}").sem, self.slot(f"at_a{s}").count)]

        def project(b):
            s = b % 2
            V.wait(*got[b])
            V.do(nc.vector.tensor_tensor, out=xa[s], in0=xa[s], in1=xy[s], op=ALU.add)
            xy_free[s] = (V.done(),)
            normed = self.layernorm(xa[s], xn, work, [V.done()], st["xn"])
            V.wait(normed)
            V.do(nc.vector.tensor_tensor, out=xa[s], in0=xa[s], in1=over(bo, 1, QT), op=ALU.add)
            PE.wait(normed)
            A.wait(*st["xnT"])
            for c in range(HC):
                PE.wait(*bank_free[0])
                for t in range(QT):
                    PE.do(nc.tensor.transpose, bank[0][:, t * P:(t + 1) * P], xn[:, t, c * P:(c + 1) * P],
                          self.ident)
                A.wait(PE.done())
                A.do(nc.scalar.copy, xnT[:, c, :], bank[0][:, :])
                bank_free[0] = (A.done(),)
            st["xn"] = (PE.done(),)
            PE.wait(A.done())
            V.wait(*proj_free[s])
            for r in range(HC + 1):
                PE.wait(*bank_free[0])
                for c in range(HC):
                    w = wq[:, c, r * P:(r + 1) * P] if r < HC else wk[:, c, :]
                    PE.do(nc.tensor.matmul, bank[0][:, :], w, xnT[:, c, :], start=c == 0, stop=c == HC - 1)
                V.wait(PE.done())
                V.do(nc.vector.scalar_tensor_tensor, out=qT[s][:, r, :] if r < HC else kT[s],
                     in0=bank[0][:, :], scalar=bq[:, r:r + 1] if r < HC else bk[:, 0:1], in1=rope,
                     op0=ALU.add, op1=ALU.mult)
                bank_free[0] = (V.done(),)
            PE.wait(*bank_free[0])
            for t in range(QT):
                for c in range(HC):
                    PE.do(nc.tensor.matmul, bank[0][:, t * P:(t + 1) * P], xnT[:, c, t * P:(t + 1) * P],
                          wv[:, c, :], start=c == 0, stop=c == HC - 1)
            st["xnT"] = (PE.done(),)
            V.wait(PE.done())
            V.do(nc.vector.tensor_tensor, out=vv[s], in0=bank[0][:, :].rearrange("p (t k) -> p t k", t=QT),
                 in1=over(bv, 1, QT), op=ALU.add)
            bank_free[0] = (V.done(),)
            ready[b] = V.done()

        units = [(b, t, h) for b in range(BATCH) for t in range(QT) for h in range(HEADS)]
        scores, masked, exped, flipped, evacuated, pv = {}, {}, {}, {}, {}, {}
        yn_free, xo_free, den_free = [(), ()], [(), ()], [(), ()]

        def order(h):
            return h % 4, h // 4

        def score(u):
            b, t, h = units[u]
            c, r = order(h)
            n = (t + 1) * P
            i = 1 + u % 3
            PE.wait(ready[b], *bank_free[i])
            rows = slice(c * HEAD, (c + 1) * HEAD)
            PE.do(nc.tensor.matmul, bank[i][:, 0:n], qT[b % 2][rows, r, t * P:(t + 1) * P],
                  kT[b % 2][rows, 0:n], start=True, stop=True)
            V.wait(PE.done())
            if u >= NS:
                V.wait(exped[u - NS])
            V.do(nc.vector.tensor_tensor_reduce, out=sc[u % NS][:, 0:n], in0=bank[i][:, 0:n],
                 in1=mask[:, SEQ - n:], scale=-SCALE, scalar=3e38, op0=ALU.add, op1=ALU.min,
                 accum_out=nb[:, u % (2 * HEADS):u % (2 * HEADS) + 1])
            bank_free[i] = (V.done(),)
            masked[u] = V.done()
            A.wait(masked[u])
            if u >= NP:
                A.wait(flipped[u - NP])
            tile = u // HEADS
            if h == 0:
                A.wait(*den_free[tile % 2])
            A.do(nc.scalar.activation, pr[u % NP][:, 0:n], sc[u % NS][:, 0:n], ACT.Exp, scale=-1.0,
                 bias=nb[:, u % (2 * HEADS):u % (2 * HEADS) + 1], accum_out=den[tile % 2][:, h:h + 1])
            exped[u] = A.done()

        def flip(u):
            b, t, h = units[u]
            n = (t + 1) * P
            i = 4 + u % 2
            PE.wait(exped[u], *bank_free[i])
            for k in range(t + 1):
                PE.do(nc.tensor.transpose, bank[i][:, k * P:(k + 1) * P], pr[u % NP][:, k * P:(k + 1) * P],
                      self.ident)
            flipped[u] = PE.done()
            if u >= 2:
                lane_wait = pv[u - 2]
            lane = A if u % 2 else V
            lane.wait(flipped[u])
            if u >= 2:
                lane.wait(lane_wait)
            if u % 2:
                A.do(nc.scalar.copy, prT[u % 2][:, 0:n], bank[i][:, 0:n])
            else:
                V.do(nc.vector.tensor_copy, prT[u % 2][:, 0:n], bank[i][:, 0:n])
            evacuated[u] = lane.done()
            bank_free[i] = (evacuated[u],)

        def weigh(u):
            b, t, h = units[u]
            c, r = order(h)
            tile = u // HEADS
            i = 6 + tile % 2
            PE.wait(evacuated[u])
            if h == 0:
                PE.wait(*bank_free[i])
            head = KV_HEADS * c + r
            for k in range(t + 1):
                PE.do(nc.tensor.matmul, bank[i][:, head * HEAD:(head + 1) * HEAD],
                      prT[u % 2][:, k * P:(k + 1) * P], vv[b % 2][:, k, c * HEAD:(c + 1) * HEAD],
                      start=k == 0, stop=k == t)
            pv[u] = PE.done()
            if h == HEADS - 1:
                finish(b, t, tile)

        def finish(b, t, tile):
            i, s = 6 + tile % 2, tile % 2
            V.wait(PE.done(), exped[tile * HEADS + HEADS - 1])
            V.do(nc.vector.reciprocal, rden, den[s])
            den_free[s] = (V.done(),)
            V.wait(V.done(), *yn_free[s])
            V.do(nc.vector.tensor_tensor, out=yn[s].rearrange("p (c r) k -> p c r k", r=4),
                 in0=bank[i][:, :].rearrange("p (c r k) -> p c r k", c=4, r=4),
                 in1=over(rden.rearrange("p (r c) -> p c r", c=4), 3, HEAD), op=ALU.mult)
            PE.wait(V.done(), *bank_free[0])
            flat = yn[s].rearrange("p h k -> p (h k)")
            bank_free[i] = (V.done(),)
            for c in range(HC):
                PE.do(nc.tensor.transpose, bank[0][:, c * P:(c + 1) * P], flat[:, c * P:(c + 1) * P], self.ident)
            yn_free[s] = (PE.done(),)
            A.wait(PE.done(), *st.get("ynT", ()))
            A.do(nc.scalar.copy, ynT, bank[0][:, :].rearrange("p (c t) -> p c t", c=HC))
            PE.wait(A.done())
            for c in range(HC):
                PE.do(nc.tensor.matmul, bank[0][:, :], ynT[:, c, :], wo[:, c, :], start=c == 0, stop=c == HC - 1)
            st["ynT"] = (PE.done(),)
            V.wait(PE.done(), *xo_free[s])
            V.do(nc.vector.tensor_tensor, out=xo[s], in0=bank[0][:, :], in1=xa[b % 2][:, t, :], op=ALU.add)
            bank_free[0] = (V.done(),)
            SP.wait(V.done())
            xo_free[s] = (self.store(f"at_o{s}", o_v[:, b * QT + t, :], xo[s]),)
            if t == QT - 1:
                xa_free[b % 2] = (V.done(),)
                proj_free[b % 2] = (PE.done(),)
                if b + 2 < BATCH:
                    load_x(b + 2)

        load_x(0)
        load_x(1)
        project(0)
        LAG = 2
        for u in range(len(units) + 2 * LAG):
            if u < len(units):
                b, t, h = units[u]
                if t == QT - 1 and h == 0 and b + 1 < BATCH:
                    project(b + 1)
                score(u)
            if 0 <= u - LAG < len(units):
                flip(u - LAG)
            if 0 <= u - LAG - 1 < len(units):
                weigh(u - LAG - 1)
        self.stage_end()
        sb.at = start

    def add_up(self, a_dram, y_dram, out_dram):
        nc, V, SP = self.nc, self.V, self.SP
        start = self.sb.at
        N = 4
        a = [self.sb.cut([QT, H]) for _ in range(N)]
        y = [self.sb.cut([QT, H]) for _ in range(N)]
        a_v = a_dram.rearrange("(b p n) h -> b p n h", p=P, n=QT)
        y_v = y_dram[0:T, :].rearrange("(b p n) h -> b p n h", p=P, n=QT)
        o_v = out_dram.rearrange("(b p n) h -> b p n h", p=P, n=QT)
        free, got = [()] * N, {}

        def fetch(b):
            SP.wait(*free[b % N])
            got[b] = (self.load(f"au_a{b % N}", a[b % N], a_v[b]), self.load(f"au_y{b % N}", y[b % N], y_v[b]))

        for b in range(N - 1):
            fetch(b)
        for b in range(BATCH):
            V.wait(*got[b])
            V.do(nc.vector.tensor_tensor, out=a[b % N], in0=a[b % N], in1=y[b % N], op=ALU.add)
            SP.wait(V.done())
            free[b % N] = (self.store(f"au_o{b % N}", o_v[b], a[b % N]),)
            if b + N - 1 < BATCH:
                fetch(b + N - 1)
        self.stage_end()
        self.sb.at = start


def build(nc, dram, stages="SFAFU"):
    with ExitStack() as ctx:
        p = Program(nc, ctx, dram)
        p.constants()
        if "S" in stages:
            p.state_space(dram["x"], dram["x1"])
        if "F" in stages:
            p.feed_forward(dram["x1"], dram["a"], dram["y"])
        if "A" in stages:
            p.attention(dram["a"], dram["y"], dram["x3"])
        if stages.count("F") == 2:
            p.feed_forward(dram["x3"], dram["a2"], dram["y2"])
        if "U" in stages:
            p.add_up(dram["a2"], dram["y2"], dram["out"])
        block = ctx.enter_context(nc.Block())
        PE, V, A, G, SP = p.lanes

        @block.tensor
        def _(eng):
            PE.play(eng)

        @block.vector
        def _(eng):
            V.play(eng)

        @block.scalar
        def _(eng):
            A.play(eng)

        @block.gpsimd
        def _(eng):
            G.play(eng)

        @block.sync
        def _(eng):
            SP.play(eng)


def rope_factor():
    f = np.float32
    inv = f(10000.0) ** (f(-2.0) * np.arange(HEAD // 2, dtype=f) / f(HEAD))
    theta = np.arange(SEQ, dtype=f)[:, None] * inv[None, :]
    both = (np.cos(theta) + np.sin(theta)).astype(f)
    return np.ascontiguousarray(np.tile(np.concatenate([both, both], axis=1).T, (P // HEAD, 1)))


def lay_out(inputs):
    g = {k: np.asarray(v) for k, v in inputs.items()}
    heads = np.arange(HEADS * HEAD).reshape(4, 4, HEAD).transpose(1, 0, 2).ravel()
    c = np.ascontiguousarray
    return {
        "x": c(g["L0_attn_a_x"].reshape(T, H)),
        "wxT": c(g["L0_attn_a_W_x"].T), "wdtT": c(g["L0_attn_a_W_dt"].T), 
        "par": c(np.stack([g["L0_attn_a_b_dt"], g["L0_attn_a_D_param"]], 1).reshape(HC, P, 2).transpose(1, 0, 2)),
        "A_log": c(g["L0_attn_a_A_log"]),
        "wqT": c(g["L0_attn_b_Wq"][heads].T), "bq": c(g["L0_attn_b_bq"][heads].reshape(HC, P).T),
        "wkT": c(g["L0_attn_b_Wk"].T), "bk": c(g["L0_attn_b_bk"].reshape(P, 1)),
        "wvT": c(g["L0_attn_b_Wv"].T), "bv": c(g["L0_attn_b_bv"]),
        "woT": c(g["L0_attn_b_Wo"].T), "bo": c(g["L0_attn_b_bo"]),
        "gate_wT": c(g["L0_ffn_gate_w"].T),
        "w_gate": c(g["L0_ffn_w_gate"]), "w_up": c(g["L0_ffn_w_up"]), "w_down": c(g["L0_ffn_w_down"]),
        "sw_gate": c(g["L0_ffn_sw_gate"]), "sw_up": c(g["L0_ffn_sw_up"]), "sw_down": c(g["L0_ffn_sw_down"]),
        "rope": rope_factor(),
    }


SCRATCH = {"bc": (BATCH, 2 * NSTATE, SEQ), "x1": (T, H), "x3": (T, H), "a": (T, H), "a2": (T, H),
           "y": (T + CAP, H), "y2": (T + CAP, H), "xn": (T + CAP, H), "tab": (SLOTS, 2)}


def declare(nc, arrays, stages="SFAFU"):
    dram = {n: nc.dram_tensor(f"in_{n}", a.shape, FP32, kind="ExternalInput").ap() for n, a in arrays.items()}
    for n, shape in SCRATCH.items():
        if n not in dram:
            dram[n] = nc.dram_tensor(f"scratch_{n}", shape, FP32).ap()
    dram["out"] = nc.dram_tensor("out", (T, H), FP32, kind="ExternalOutput").ap()
    build(nc, dram, stages)


def kernel(**inputs):
    import concourse.bacc as bacc
    from concourse.bass_utils import run_bass_kernel_spmd

    arrays = lay_out(inputs)
    nc = bacc.Bacc("TRN2", target_bir_lowering=False, num_devices=1)
    declare(nc, arrays)
    r = run_bass_kernel_spmd(nc, [{f"in_{n}": a for n, a in arrays.items()}], core_ids=[0])
    return r.results[0]["out"].reshape(BATCH, SEQ, H)
```

```python
from contextlib import ExitStack

import numpy as np

import concourse.bass as bass
from concourse import mybir

FP32 = mybir.dt.float32
BF16 = mybir.dt.bfloat16
I32 = mybir.dt.int32
ALU = mybir.AluOpType
ACT = mybir.ActivationFunctionType
AXIS_X = mybir.AxisListType.X

P = 128
BATCH, SEQ, H = 8, 512, 512
T = BATCH * SEQ
NT = T // P
QT = SEQ // P
HC = H // P
NSTATE, DT_RANK = 16, 128
HEADS, KV_HEADS, HEAD = 16, 4, 32
E, TOPK, INTER, CAP = 64, 6, 352, 64
SHARED = 2 * INTER
SLOTS = E * CAP
EPS = 1e-5
NEG = -1e30
BANK = 512
ARENA = 52800


class Lane:

    def __init__(self, nc, name):
        self.nc, self.name, self.queue, self.waited = nc, name, [], {}
        self.sem, self.count, self.sems = None, 0, 0
        self.last, self.mark = None, None

    def new_count(self, ctx):
        self.sem = ctx.enter_context(self.nc.semaphore(f"{self.name}_{self.sems}"))
        self.count, self.sems = 0, self.sems + 1

    def do(self, method, *args, **kw):
        self.last = [method, args, kw, None]
        self.queue.append(self.last)

    def done(self):
        if self.last[3] is None:
            self.count += 1
            self.last[3] = (self.sem, 1)
            self.mark = (self.sem, self.count)
        return self.mark

    def wait(self, *marks):
        for sem, value in marks:
            if self.waited.get(sem.name, 0) < value:
                self.waited[sem.name] = value
                self.queue.append(["wait", sem, value, None])

    def dma(self, method, slot, *args, **kw):
        slot.count += 16
        self.queue.append([method, args, kw, (slot.sem, 16)])
        return (slot.sem, slot.count)

    def play(self, engine):
        for method, args, kw, inc in self.queue:
            if isinstance(method, str):
                engine.wait_ge(args, kw)
            elif inc is None:
                method(*args, **kw)
            else:
                method(*args, **kw).then_inc(*inc)


class Slot:

    def __init__(self, ctx, nc, name):
        self.sem, self.count = ctx.enter_context(nc.semaphore(name)), 0


class Arena:

    def __init__(self, base):
        self.base, self.at = base, 0

    def cut(self, shape, dt=FP32):
        n = int(np.prod(shape))
        words = n if dt in (FP32, I32) else (n + 1) // 2
        words = (words + 7) // 8 * 8
        assert self.at + words <= ARENA, (self.at, words)
        view = self.base[:, self.at:self.at + words]
        self.at += words
        if dt != FP32:
            view = view.bitcast(dt)
        view = view[:, 0:n]
        if len(shape) == 2:
            view = view.rearrange("p (a b) -> p a b", a=shape[0])
        if len(shape) == 3:
            view = view.rearrange("p (a b c) -> p a b c", a=shape[0], b=shape[1])
        return view


def over(ap, axis, n):
    v = ap.unsqueeze(axis)
    shape = list(v.shape)
    shape[axis] = n
    return v.to_broadcast(shape)


class Program:
    EARLY = (1, 2, 1, 2)

    def __init__(self, nc, ctx, dram):
        self.nc, self.ctx, self.d = nc, ctx, dram
        base = ctx.enter_context(nc.sbuf_tensor("arena", [P, ARENA], FP32))
        self.sb = Arena(base)
        self.bank = [ctx.enter_context(nc.psum_tensor(f"bank{i}", [P, BANK], FP32)) for i in range(8)]
        self.PE, self.V, self.A, self.G, self.SP = (Lane(nc, n) for n in ("pe", "dve", "act", "pool", "sp"))
        self.lanes = [self.PE, self.V, self.A, self.G, self.SP]
        for lane in self.lanes:
            lane.new_count(ctx)
        self.slots, self.open = {}, []

    def slot(self, name):
        if name not in self.slots:
            self.slots[name] = Slot(self.ctx, self.nc, name)
        return self.slots[name]

    def load(self, name, out, in_):
        mark = self.SP.dma(self.nc.sync.dma_start, self.slot(name), out, in_)
        self.open.append(mark)
        return mark

    store = load

    def stage_end(self):
        marks = [lane.done() for lane in self.lanes[:4] if lane.last]
        last = {}
        for sem, value in self.open:
            last[sem.name] = (sem, max(value, last.get(sem.name, (sem, 0))[1]))
        self.open = []
        for lane in self.lanes:
            lane.wait(*marks, *last.values())
        for lane in self.lanes[:4]:
            lane.new_count(self.ctx)

    def constants(self):
        nc, G, V = self.nc, self.G, self.V
        self.ident = self.sb.cut([P])
        self.half = self.sb.cut([8])
        G.do(nc.gpsimd.memset, self.ident, 0.0)
        G.do(nc.gpsimd.memset, self.half, -0.5)
        G.wait(G.done())
        G.do(nc.gpsimd.affine_select, out=self.ident, in_=self.ident, compare_op=ALU.not_equal, fill=1.0,
             base=0, pattern=[[-1, P]], channel_multiplier=1)
        self.ready = G.done()
        for lane in (self.PE, V, self.A, self.SP, G):
            lane.wait(self.ready)

    def layernorm(self, x, xn, work, x_ready, xn_free=()):
        nc, V, G = self.nc, self.V, self.G
        n = x.shape[1]
        stats, mv, rstd = work
        V.wait(*x_ready)
        for i in range(n):
            V.do(nc.vector.bn_stats, out=stats[:, i, :], in_=x[:, i, :])
        V.wait(V.done())
        for i in range(n):
            V.do(nc.vector.bn_aggr, out=mv[:, i, :], in_=stats[:, i, :])
        G.wait(V.done())
        G.do(nc.gpsimd.tensor_scalar, rstd, mv[:, :, 1], EPS, None, ALU.add)
        G.wait(G.done())
        G.do(nc.gpsimd.tensor_tensor, out=rstd, in0=rstd, in1=self.half[:, 0:n], op=ALU.pow)
        V.wait(G.done(), *xn_free)
        for i in range(n):
            V.do(nc.vector.tensor_scalar, xn[:, i, :], x[:, i, :], mv[:, i, 0:1], rstd[:, i:i + 1],
                 ALU.subtract, ALU.mult)
        return V.done()

    def norm_work(self, n):
        return self.sb.cut([n, 6]), self.sb.cut([n, 2]), self.sb.cut([n])


    def state_space(self, x_dram, out_dram):
        nc, d = self.nc, self.d
        PE, V, A, G, SP = self.lanes
        sb, bank = self.sb, self.bank
        start = sb.at
        NG = 4
        GROUPS = NSTATE // NG
        RING = 3
        HB = 4
        wx = sb.cut([HC, DT_RANK + 2 * NSTATE])
        wdt = sb.cut([H])
        par = sb.cut([HC, 2])
        alog = sb.cut([HC, NSTATE])
        diag = sb.cut([HC, P])
        xin = [sb.cut([QT, H]) for _ in range(2)]
        xn = sb.cut([QT, H])
        xnT = [sb.cut([HC, SEQ]) for _ in range(2)]
        dt = [sb.cut([HC, SEQ]) for _ in range(2)]
        dtx = [sb.cut([HC, SEQ]) for _ in range(2)]
        soft = sb.cut([HC, SEQ])
        dtr = sb.cut([SEQ])
        bcs = sb.cut([SEQ])
        bb = [sb.cut([NG, SEQ]) for _ in range(RING)]
        cb = [sb.cut([NG, SEQ]) for _ in range(RING)]
        da = [sb.cut([NG, SEQ]) for _ in range(2)]
        hb = [sb.cut([NG, SEQ]) for _ in range(HB)]
        work = self.norm_work(QT)
        x_v = x_dram.rearrange("(n p) h -> p n h", p=P)
        o_v = out_dram.rearrange("(n p) h -> p n h", p=P)
        bc_dram = d["bc"]

        w_in = [self.load("ss_w", wx, d["wxT"].rearrange("(c p) k -> p c k", p=P)),
                self.load("ss_w", wdt, d["wdtT"]),
                self.load("ss_w", par, d["par"]),
                self.load("ss_w", alog, d["A_log"].rearrange("(c p) n -> p c n", p=P))][-1:]

        xload, prepared, bcload, ring_free = {}, {}, {}, [()] * RING
        spare_free, nspare = [()] * 8, [0]

        def spare():
            i = 4 + nspare[0] % 4
            nspare[0] += 1
            PE.wait(*spare_free[i])
            return i

        xin_free, xnT_free, dt_free = [(), ()], [(), ()], [(), ()]
        y_free = [()] * QT
        st = {"soft": (), "dtr": (), "bcs": (), "xn": ()}

        def load_x(b):
            SP.wait(*xin_free[b % 2])
            xload[b] = self.load(f"ss_x{b % 2}", xin[b % 2], x_v[:, b * QT:(b + 1) * QT, :])

        load_x(0)
        for lane in (PE, V, A, G):
            lane.wait(*w_in)
        A.do(nc.scalar.activation, alog, alog, ACT.Exp)
        V.wait(A.done())
        V.do(nc.vector.tensor_scalar, alog, alog, -1.0, None, ALU.mult)
        for t in da:
            V.do(nc.vector.memset, t[:, :, 0:1], 0.0)
        for c in range(HC):
            V.do(nc.vector.tensor_scalar, diag[:, c, :], self.ident, par[:, c, 1:2], None, ALU.mult)
        A.wait(V.done())
        PE.wait(V.done())

        def prepare(b):
            s = b % 2
            stats, mv, rstd = work
            V.wait(xload[b])
            for i in range(QT):
                V.do(nc.vector.bn_stats, out=stats[:, i, :], in_=xin[s][:, i, :])
            V.wait(V.done())
            for i in range(QT):
                V.do(nc.vector.bn_aggr, out=mv[:, i, :], in_=stats[:, i, :])
            G.wait(V.done())
            G.do(nc.gpsimd.tensor_scalar, rstd, mv[:, :, 1], EPS, None, ALU.add)
            G.wait(G.done())
            G.do(nc.gpsimd.tensor_tensor, out=rstd, in0=rstd, in1=self.half[:, 0:QT], op=ALU.pow)
            scaled = G.done()
            yield
            V.wait(scaled, *st["xn"])
            for i in range(QT):
                V.do(nc.vector.tensor_scalar, xn[:, i, :], xin[s][:, i, :], mv[:, i, 0:1], rstd[:, i:i + 1],
                     ALU.subtract, ALU.mult)
            normed = V.done()
            yield
            PE.wait(normed)
            A.wait(*xnT_free[s])
            for c in range(HC):
                i = spare()
                for t in range(QT):
                    PE.do(nc.tensor.transpose, bank[i][:, t * P:(t + 1) * P], xn[:, t, c * P:(c + 1) * P],
                          self.ident)
                A.wait(PE.done())
                A.do(nc.scalar.copy, xnT[s][:, c, :], bank[i][:, :])
                spare_free[i] = (A.done(),)
                if c % 2:
                    yield
            st["xn"] = (PE.done(),)
            turned = A.done()
            PE.wait(turned)
            i = spare()
            for c in range(HC):
                PE.do(nc.tensor.matmul, bank[i][:, :], wx[:, c, 0:DT_RANK], xnT[s][:, c, :],
                      start=c == 0, stop=c == HC - 1)
            A.wait(PE.done(), *st["dtr"])
            A.do(nc.scalar.copy, dtr, bank[i][:, :])
            ranked = A.done()
            spare_free[i] = (ranked,)
            i = spare()
            R = 2 * NSTATE
            for c in range(HC):
                PE.do(nc.tensor.matmul, bank[i][0:R, :], wx[:, c, DT_RANK:], xnT[s][:, c, :],
                      start=c == 0, stop=c == HC - 1)
            A.wait(PE.done(), *st["bcs"])
            A.do(nc.scalar.copy, bcs[0:R, :], bank[i][0:R, :])
            spare_free[i] = (A.done(),)
            SP.wait(A.done())
            stored = self.store("ss_bc", bc_dram[b, :, :], bcs[0:R, :])
            st["bcs"] = (stored,)
            prepared[b] = [stored]
            yield
            PE.wait(ranked)
            A.wait(*dt_free[s], *st["soft"])
            for c in range(HC):
                i = spare()
                PE.do(nc.tensor.matmul, bank[i][:, :], wdt[:, c * P:(c + 1) * P], dtr, start=True, stop=True)
                A.wait(PE.done())
                A.do(nc.scalar.activation, soft[:, c, :], bank[i][:, :], ACT.Abs, bias=par[:, c, 0:1])
                A.do(nc.scalar.activation, dt[s][:, c, :], bank[i][:, :], ACT.Relu, bias=par[:, c, 0:1])
                spare_free[i] = (A.done(),)
                if c % 2:
                    yield
            st["dtr"] = (PE.done(),)
            A.wait(A.done())
            A.do(nc.scalar.activation, soft, soft, ACT.Exp, scale=-1.0)
            A.wait(A.done())
            yield
            A.do(nc.scalar.activation, soft, soft, ACT.Ln, bias=1.0)
            logged = A.done()
            yield
            V.wait(logged)
            V.do(nc.vector.tensor_tensor, out=dt[s], in0=dt[s], in1=soft, op=ALU.add)
            st["soft"] = (V.done(),)
            yield
            G.wait(*st["soft"])
            G.do(nc.gpsimd.tensor_tensor, out=dtx[s], in0=dt[s], in1=xnT[s], op=ALU.mult)
            prepared[b].append(G.done())
            yield

        def load_bc(n):
            b, g = divmod(n, GROUPS)
            r = n % RING
            SP.wait(prepared[b][0], *ring_free[r])
            for buf, row, name in ((bb, 0, "b"), (cb, NSTATE, "c")):
                src = bc_dram[b, row + g * NG:row + (g + 1) * NG, :].partition_broadcast(P)
                bcload[b, g, name] = self.load(f"ss_{name}{r}", buf[r], src)

        for _ in prepare(0):
            pass
        load_x(1)
        next_bc = 0
        steps = [(b, g, c) for b in range(BATCH) for g in range(GROUPS) for c in range(HC)]
        scanned, summed, multiplied = {}, {}, {}
        coming = iter(())
        for k in range(len(steps) + 1):
            if k < len(steps):
                b, g, c = steps[k]
                s, r = b % 2, (b * GROUPS + g) % RING
                if c == 1 or k == 0:
                    while next_bc < BATCH * GROUPS and next_bc < b * GROUPS + g + RING and next_bc // GROUPS in prepared:
                        load_bc(next_bc)
                        next_bc += 1
                if g == 0 and c == 0:
                    A.wait(prepared[b][1])
                    G.wait(prepared[b][1])
                if k >= 2:
                    A.wait(scanned[k - 2])
                for n in range(NG):
                    A.do(nc.scalar.activation, da[k % 2][:, n, 1:SEQ], dt[s][:, c, 1:SEQ], ACT.Exp,
                         scale=alog[:, c, g * NG + n:g * NG + n + 1])
                decay = A.done()
                G.wait(bcload[b, g, "b"])
                if k >= HB:
                    G.wait(summed[k - HB])
                G.do(nc.gpsimd.tensor_tensor, out=hb[k % HB], in0=over(dtx[s][:, c, :], 1, NG), in1=bb[r],
                     op=ALU.mult)
                inflow = G.done()
                if g == GROUPS - 1 and c == HC - 1:
                    dt_free[s] = (decay, inflow)
                V.wait(decay, inflow)
                flat = "p a b -> p (a b)"
                V.do(nc.vector.tensor_tensor_scan, out=hb[k % HB].rearrange(flat), data0=da[k % 2].rearrange(flat),
                     data1=hb[k % HB].rearrange(flat), initial=0.0, op0=ALU.mult, op1=ALU.add)
                scanned[k] = V.done()
            if k > 0:
                next(coming, None)
                b, g, c = steps[k - 1]
                s, r = b % 2, (b * GROUPS + g) % RING
                V.wait(scanned[k - 1], bcload[b, g, "c"])
                w = hb[(k - 1) % HB]
                V.do(nc.vector.tensor_tensor, out=w, in0=w, in1=cb[r], op=ALU.mult)
                multiplied[k - 1] = V.done()
                chan = slice(c * P, (c + 1) * P)
                first = g == 0 and c == 0
                for t in range(QT):
                    toks = slice(t * P, (t + 1) * P)
                    if first:
                        PE.wait(*y_free[t])
                    if g == 0:
                        PE.do(nc.tensor.matmul, bank[t][:, chan], xnT[s][:, c, toks], diag[:, c, :],
                              start=first, stop=False, skip_group_check=True)
                PE.wait(multiplied[k - 1])
                for n in range(NG):
                    for t in range(QT):
                        PE.do(nc.tensor.matmul, bank[t][:, chan], w[:, n, t * P:(t + 1) * P], self.ident,
                              is_transpose=True, start=False,
                              stop=g == GROUPS - 1 and n == NG - 1, skip_group_check=True)
                summed[k - 1] = PE.done()
                if c == HC - 1:
                    ring_free[r] = (multiplied[k - 1], inflow)
                    if g == 0:
                        xnT_free[s] = (summed[k - 1],)
                        if b + 1 < BATCH:
                            coming = prepare(b + 1)
                if g == GROUPS - 1 and c == HC - 1:
                    for t in range(QT):
                        V.wait(summed[k - 1])
                        V.do(nc.vector.tensor_tensor, out=xin[s][:, t, :], in0=xin[s][:, t, :], in1=bank[t][:, :],
                             op=ALU.add)
                        y_free[t] = (V.done(),)
                    SP.wait(V.done())
                    xin_free[s] = (self.store(f"ss_out{s}", o_v[:, b * QT:(b + 1) * QT, :], xin[s]),)
                    if b + 2 < BATCH:
                        load_x(b + 2)
        self.stage_end()
        sb.at = start


    def feed_forward(self, x_dram, a_dram, y_dram):
        nc, d = self.nc, self.d
        PE, V, A, G, SP = self.lanes
        sb, bank = self.sb, self.bank
        start = sb.at
        xn_dram, tab = d["xn"], d["tab"]
        x_v = x_dram.rearrange("(n p) h -> p n h", p=P)
        n_v = xn_dram[0:T, :].rearrange("(n p) h -> p n h", p=P)
        y_v = y_dram[0:T, :].rearrange("(n p) h -> p n h", p=P)
        PAIR = 2 * CAP
        NPAIR = E // 2
        NQ = T // BANK
        IC = 3
        last = INTER - 2 * P
        SC = (SHARED + P - 1) // P
        last_s = SHARED - (SC - 1) * P
        OUT = 3

        xnT = sb.cut([HC, T])
        ids = sb.cut([NPAIR], I32)
        wts = sb.cut([NPAIR])
        ids1 = sb.cut([E], I32)
        swg, swu = sb.cut([HC, SHARED]), sb.cut([HC, SHARED])
        swd = sb.cut([SC, H])
        shT = sb.cut([SC, BANK])
        ssg = sb.cut([BANK])
        so = [sb.cut([H]) for _ in range(OUT)]
        xe = [sb.cut([H]) for _ in range(2)]

        def weights():
            return sb.cut([HC, INTER]), sb.cut([HC, INTER]), sb.cut([IC, H])

        ring = [weights() for _ in range(2)]
        region = sb.at

        gw = sb.cut([HC, E])
        tri = sb.cut([P], BF16)
        ones = sb.cut([P], BF16)
        trif = sb.cut([P])
        token = sb.cut([NT])
        first = sb.cut([E])
        pad = sb.cut([E, 2])
        xt = [sb.cut([QT, H]) for _ in range(2)]
        xn = sb.cut([QT, H])
        work = self.norm_work(QT)
        score = sb.cut([QT, E + 2])
        marked = sb.cut([QT, E + 2])
        mask = sb.cut([QT, E], BF16)
        seen = sb.cut([E], BF16)
        small = sb.cut([3, QT])
        top = sb.cut([QT, 8])
        six = sb.cut([QT, 8])
        valid = sb.cut([QT, E])
        code = sb.cut([QT, E])
        best = sb.cut([QT, 8])
        where = [sb.cut([QT, 8], I32) for _ in range(2)]
        equal = sb.cut([QT * TOPK, E])
        pair = [sb.cut([QT, TOPK, 2]) for _ in range(2)]
        tab2 = sb.cut([NPAIR, 2])
        tab1 = sb.cut([E, 2])
        zero = sb.cut([H])

        w_in = self.load("ff_w", gw, d["gate_wT"].rearrange("(p c) e -> p c e", c=HC))
        G.do(nc.gpsimd.memset, trif, 1.0)
        G.do(nc.gpsimd.memset, ones, 1.0)
        G.do(nc.gpsimd.memset, seen, 0.0)
        G.do(nc.gpsimd.memset, six, -1.0)
        G.do(nc.gpsimd.memset, score, -1.0)
        G.do(nc.gpsimd.memset, pad, 0.0)
        G.do(nc.gpsimd.memset, zero, 0.0)
        G.do(nc.gpsimd.iota, token, pattern=[[P, NT]], base=0, channel_multiplier=1,
             allow_small_or_imprecise_dtypes=True)
        G.do(nc.gpsimd.iota, first, pattern=[[-CAP, E]], base=SLOTS, channel_multiplier=0,
             allow_small_or_imprecise_dtypes=True)
        G.wait(G.done())
        G.do(nc.gpsimd.affine_select, out=trif, in_=trif, compare_op=ALU.is_gt, fill=0.0, base=0,
             pattern=[[1, P]], channel_multiplier=-1)
        G.do(nc.gpsimd.iota, pad[:, :, 0], pattern=[[0, E]], base=T, channel_multiplier=1,
             allow_small_or_imprecise_dtypes=True)
        G.wait(G.done())
        G.do(nc.gpsimd.tensor_copy, tri, trif)
        set_up = G.done()

        x_free, xload = [(), ()], {}

        def load_x(q):
            SP.wait(*x_free[q % 2])
            xload[q] = self.load(f"ff_x{q % 2}", xt[q % 2], x_v[:, q * QT:(q + 1) * QT, :])

        load_x(0)
        load_x(1)
        self.load("ff_sw", swg, d["sw_gate"].rearrange("(p c) i -> p c i", c=HC))
        self.load("ff_sw", swu, d["sw_up"].rearrange("(p c) i -> p c i", c=HC))
        self.load("ff_sw", swd[:, 0:SC - 1, :], d["sw_down"][0:(SC - 1) * P, :].rearrange("(j p) h -> p j h", p=P))
        sw_in = self.load("ff_sw", swd[0:last_s, SC - 1, :], d["sw_down"][(SC - 1) * P:, :])
        for lane in (PE, V, SP):
            lane.wait(set_up)
        PE.wait(w_in)
        padded = self.store("ff_pad", tab.rearrange("(e c) t -> c e t", c=CAP), pad[0:CAP])
        self.store("ff_pad2", xn_dram[T:T + CAP, :], zero[0:CAP, :])
        self.store("ff_pad2", y_dram[T:T + CAP, :], zero[0:CAP, :])
        pads = len(self.open) - 1

        sh = {"h": (), "so_free": [()] * OUT,
              "gu": (), "h_free": (), "out": (), "stores": []}
        quad_ready = {}

        def shared_up(q, j):
            m = P if j < SC - 1 else last_s
            toks = slice(q * BANK, (q + 1) * BANK)
            PE.wait(sw_in, *quad_ready[q], *sh["gu"])
            for w, bk in ((swg, 5), (swu, 6)):
                for c in range(HC):
                    PE.do(nc.tensor.matmul, bank[bk][0:m, :], w[:, c, j * P:j * P + m], xnT[:, c, toks],
                          start=c == 0, stop=c == HC - 1)
                if bk == 5:
                    A.wait(PE.done(), *sh["gu"])
                    A.do(nc.scalar.activation, ssg[0:m, :], bank[5][0:m, :], ACT.Silu)
            V.wait(A.done(), PE.done(), *sh["h_free"])
            V.do(nc.vector.tensor_tensor, out=shT[0:m, j, :], in0=ssg[0:m, :], in1=bank[6][0:m, :],
                 op=ALU.mult)
            sh["gu"] = sh["h"] = (V.done(),)

        def shared_down(q, t):
            i = q * QT + t
            s = i % OUT
            shared_store()
            PE.wait(*sh["h"], *sh["out"])
            for j in range(SC):
                m = P if j < SC - 1 else last_s
                PE.do(nc.tensor.matmul, bank[7][:, :], shT[0:m, j, t * P:(t + 1) * P], swd[0:m, j, :],
                      start=j == 0, stop=j == SC - 1)
            if t == QT - 1:
                sh["h_free"] = (PE.done(),)
            V.wait(PE.done(), *sh["so_free"][s])
            V.do(nc.vector.tensor_copy, so[s], bank[7][:, :])
            sh["out"] = (V.done(),)
            sh["stores"].append((i, s, V.done()))

        def shared_store():
            for i, s, added in sh["stores"]:
                SP.wait(added)
                sh["so_free"][s] = (self.store(f"ff_so{s}", a_dram[i * P:(i + 1) * P, :], so[s]),)
            sh["stores"] = []

        units = []
        for q in range(NQ):
            units += [(shared_up, q, j) for j in range(SC)] + [(shared_down, q, t) for t in range(QT)]
        units.reverse()

        def spend(n):
            while n > 0 and units and units[-1][1] in quad_ready:
                f, q, j = units.pop()
                f(q, j)
                n -= 1

        st = {"xn": (), "t": [(), ()], "logits": (), "pos": (), "score": (), "where": [(), ()], "mask": ()}

        def route(q):
            normed = self.layernorm(xt[q % 2], xn, work, [xload[q]], st["xn"])
            SP.wait(xload[q])
            copied = self.store(f"ff_y{q % 2}", y_v[:, q * QT:(q + 1) * QT, :], xt[q % 2])
            x_free[q % 2] = (normed, copied)
            SP.wait(normed)
            stored = self.store("ff_n", n_v[:, q * QT:(q + 1) * QT, :], xn)
            yield
            cols = xn.rearrange("p t (m c) -> p t c m", c=HC)
            for c in range(HC):
                b = 3 * (c % 2)
                PE.wait(normed, *st["t"][c % 2])
                for t in range(QT):
                    PE.do(nc.tensor.transpose, bank[b][:, t * P:(t + 1) * P], cols[:, t, c, :], self.ident)
                A.wait(PE.done())
                A.do(nc.scalar.copy, xnT[:, c, q * BANK:(q + 1) * BANK], bank[b][:, :])
                st["t"][c % 2] = (A.done(),)
            st["xn"] = (PE.done(), stored)
            quad_ready[q] = (A.done(),)
            if q + 2 < NQ:
                load_x(q + 2)
            yield
            PE.wait(A.done(), *st["logits"])
            logits = bank[1][:, 0:QT * E].rearrange("p (t e) -> p t e", t=QT)
            for t in range(QT):
                for c in range(HC):
                    PE.do(nc.tensor.matmul, logits[:, t, :], xnT[:, c, q * BANK + t * P:q * BANK + (t + 1) * P],
                          gw[:, c, :], start=c == 0, stop=c == HC - 1)
            V.wait(PE.done(), *st["score"])
            V.do(nc.vector.tensor_reduce, out=small[:, 0, :], in_=logits, axis=AXIS_X, op=ALU.max)
            V.wait(V.done())
            own = score[:, :, 0:E]
            V.do(nc.vector.tensor_tensor, out=own, in0=logits, in1=over(small[:, 0, :], 2, E), op=ALU.subtract)
            st["logits"] = (V.done(),)
            A.wait(V.done())
            A.do(nc.scalar.activation, own, own, ACT.Exp)
            exped = A.done()
            yield
            V.wait(exped)
            V.do(nc.vector.tensor_reduce, out=small[:, 1, :], in_=own, axis=AXIS_X, op=ALU.add)
            V.wait(V.done())
            V.do(nc.vector.reciprocal, small[:, 2, :], small[:, 1, :])
            V.wait(V.done())
            V.do(nc.vector.tensor_tensor, out=own, in0=own, in1=over(small[:, 2, :], 2, E), op=ALU.mult)
            V.wait(V.done())
            for t in range(QT):
                V.do(nc.vector.max, out=top[:, t, :], in_=score[:, t, 0:E])
            V.wait(V.done())
            V.do(nc.vector.tensor_copy, six[:, :, 0:TOPK], top[:, :, 0:TOPK])
            V.wait(V.done())
            for t in range(QT):
                V.do(nc.vector.match_replace, out=marked[:, t, :], in_to_replace=six[:, t, :],
                     in_values=score[:, t, :], imm_value=-2.0)
            V.wait(V.done(), *st["pos"])
            V.do(nc.vector.tensor_scalar, mask, marked[:, :, 0:E], -2.0, None, ALU.is_equal)
            masked = V.done()
            yield
            PE.wait(masked, *st["pos"])
            pos = bank[2][:, 0:QT * E].rearrange("p (t e) -> p t e", t=QT)
            for t in range(QT):
                PE.do(nc.tensor.matmul, pos[:, t, :], tri, mask[:, t, :], start=True, stop=False)
                for before in range(t):
                    PE.do(nc.tensor.matmul, pos[:, t, :], ones, mask[:, before, :], start=False, stop=False)
                PE.do(nc.tensor.matmul, pos[:, t, :], ones, seen, start=False, stop=True)
            counted = PE.done()
            V.wait(counted)
            V.do(nc.vector.tensor_scalar, valid, pos, float(CAP), None, ALU.is_lt)
            V.do(nc.vector.tensor_scalar, code, pos, -1.0, None, ALU.mult)
            st["pos"] = (V.done(),)
            V.wait(V.done())
            V.do(nc.vector.tensor_tensor, out=valid, in0=valid, in1=mask, op=ALU.mult)
            V.do(nc.vector.tensor_tensor, out=code, in0=code, in1=over(first, 1, QT), op=ALU.add)
            for t in range(QT):
                V.do(nc.vector.tensor_tensor, out=seen, in0=seen, in1=mask[:, t, :], op=ALU.add)
                V.wait(V.done())
            st["pos"] = (V.done(),)
            V.do(nc.vector.tensor_tensor, out=code, in0=code, in1=valid, op=ALU.mult)
            V.wait(V.done())
            for t in range(QT):
                V.do(nc.vector.max, out=best[:, t, :], in_=code[:, t, :])
            coded = V.done()
            yield
            s = q % 2
            V.wait(coded, *st["where"][s])
            V.do(nc.vector.tensor_scalar, where[s], best, -1.0, float(SLOTS), ALU.mult, ALU.add)
            for t in range(QT):
                V.do(nc.vector.tensor_tensor, out=equal[:, t * TOPK:(t + 1) * TOPK, :],
                     in0=over(code[:, t, :], 1, TOPK), in1=over(best[:, t, 0:TOPK], 2, E), op=ALU.is_equal)
            V.wait(V.done())
            for t in range(QT):
                V.do(nc.vector.tensor_tensor, out=equal[:, t * TOPK:(t + 1) * TOPK, :],
                     in0=equal[:, t * TOPK:(t + 1) * TOPK, :], in1=over(score[:, t, 0:E], 1, TOPK), op=ALU.mult)
            V.wait(V.done())
            V.do(nc.vector.tensor_reduce, out=pair[s].rearrange("p t k w -> p (t k) w")[:, :, 1], in_=equal,
                 axis=AXIS_X, op=ALU.add)
            V.do(nc.vector.tensor_copy, pair[s][:, :, :, 0], over(token[:, q * QT:(q + 1) * QT], 2, TOPK))
            st["score"] = (V.done(),)
            G.wait(V.done(), padded)
            for t in range(QT):
                for k in range(TOPK):
                    mark = G.dma(nc.gpsimd.indirect_dma_start, self.slot(f"ff_s{s}"), out=tab[:, :],
                                 out_offset=bass.IndirectOffsetOnAxis(ap=where[s][:, t, k:k + 1], axis=0),
                                 in_=pair[s][:, t, k, :], in_offset=None, bounds_check=SLOTS - 1,
                                 oob_is_err=False)
            self.open.append(mark)
            st["where"][s] = (mark,)
            st["table"] = st["where"][0] + st["where"][1]
            yield

        wload, up_free, down_free = {}, [()] * 4, [()] * 4

        def load_up(e):
            r = e % 4
            SP.wait(*up_free[r])
            self.load(f"ff_w{r}", ring[r][0], d["w_gate"][e].rearrange("(p c) i -> p c i", c=HC))
            wload[e, "up"] = self.load(f"ff_w{r}", ring[r][1], d["w_up"][e].rearrange("(p c) i -> p c i", c=HC))

        def load_down(e):
            r = e % 4
            dn = ring[r][2]
            SP.wait(*down_free[r])
            self.load(f"ff_d{r}", dn[:, 0:2, :], d["w_down"][e, 0:2 * P, :].rearrange("(j p) h -> p j h", p=P))
            wload[e, "down"] = self.load(f"ff_d{r}", dn[0:last, 2, :], d["w_down"][e, 2 * P:, :])

        routes = [route(q) for q in range(NQ)]
        next(routes[0])
        next(routes[0])
        for q in range(NQ):
            for step in (3, 4, 5, 6):
                next(routes[q])
                if step > 4 and q + 1 < NQ:
                    next(routes[q + 1])
                spend(self.EARLY[step - 3])
            if q == 1:
                for e in range(2):
                    load_up(e)
                    load_down(e)
        V.do(nc.vector.memset, bank[3][last:P, :], 0.0)
        routed = (V.done(), PE.done(), A.done(), G.done()) + st["xn"]
        SP.wait(*st["table"])
        self.load("ff_tab", tab2, tab.rearrange("(q c) t -> c q t", c=PAIR))
        read = self.load("ff_tab", tab1[0:CAP], tab.rearrange("(e c) t -> c e t", c=CAP))
        spend(2)
        V.wait(read)
        V.do(nc.vector.tensor_copy, ids, tab2[:, :, 0])
        V.do(nc.vector.tensor_copy, wts, tab2[:, :, 1])
        V.do(nc.vector.tensor_copy, ids1[0:CAP, :], tab1[0:CAP, :, 0])
        listed = V.done()

        sb.at = region
        ring += [weights() for _ in range(2)]
        xeT = [sb.cut([HC, PAIR]) for _ in range(2)]
        sg, hid = sb.cut([INTER]), sb.cut([INTER])
        hT = [sb.cut([IC, PAIR]) for _ in range(2)]
        ye = [sb.cut([H]) for _ in range(2)]
        for lane in (SP, V, A, G, PE):
            lane.wait(*routed, listed, self.open[pads])
        G.wait(*x_free[0], *x_free[1], *st["xn"], self.open[pads])
        xe_free, xeT_free, hT_free, ye_free = [(), ()], [(), ()], [(), ()], [(), ()]
        o = {"t": (), "gu": (), "sg": (), "flip": (), "y": (), "sum": ()}
        xeload, turned, hidden, flipped = {}, {}, {}, {}

        def gather(p):
            s = p % 2
            G.wait(*xe_free[s])
            xeload[p] = G.dma(nc.gpsimd.indirect_dma_start, self.slot(f"ff_xe{s}"), out=xe[s],
                              out_offset=None, in_=xn_dram[:, :],
                              in_offset=bass.IndirectOffsetOnAxis(ap=ids[:, p:p + 1], axis=0),
                              bounds_check=T + CAP - 1, oob_is_err=True)
            self.open.append(xeload[p])

        def turn(p):
            PE.wait(xeload[p], *o["t"])
            cols = xe[p % 2].rearrange("p (m c) -> p c m", c=HC)
            for c in range(HC):
                PE.do(nc.tensor.transpose, bank[0][:, c * PAIR:(c + 1) * PAIR], cols[:, c, :], self.ident)
            xe_free[p % 2] = (PE.done(),)
            V.wait(PE.done(), *xeT_free[p % 2])
            V.do(nc.vector.tensor_copy, xeT[p % 2], bank[0][:, :].rearrange("p (c t) -> p c t", c=HC))
            turned[p] = V.done()
            o["t"] = (V.done(),)

        def up(p):
            PE.wait(wload[2 * p, "up"], wload[2 * p + 1, "up"], turned[p], *o["gu"])
            for w in range(2):
                for c in range(HC):
                    for half in range(2):
                        mine = slice(half * CAP, (half + 1) * CAP)
                        PE.do(nc.tensor.matmul, bank[1 + w][mine, 0:INTER], xeT[p % 2][:, c, mine],
                              ring[(2 * p + half) % 4][w][:, c, :], start=c == 0, stop=c == HC - 1)
                if w == 0:
                    A.wait(PE.done(), *o["sg"])
                    A.do(nc.scalar.activation, sg, bank[1][:, 0:INTER], ACT.Silu)
            xeT_free[p % 2] = (PE.done(),)
            for e in (2 * p, 2 * p + 1):
                up_free[e % 4] = (PE.done(),)
                if e + 4 < E:
                    load_up(e + 4)
            V.wait(A.done(), PE.done(), *o["flip"])
            V.do(nc.vector.tensor_tensor, out=hid, in0=sg, in1=bank[2][:, 0:INTER], op=ALU.mult)
            o["gu"] = o["sg"] = (V.done(),)
            hidden[p] = V.done()

        def flip(p):
            PE.wait(hidden[p], *o.get("flipped", ()))
            for j in range(IC):
                m = P if j < 2 else last
                PE.do(nc.tensor.transpose, bank[3][0:m, j * PAIR:(j + 1) * PAIR], hid[:, j * P:j * P + m],
                      self.ident)
            o["flip"] = (PE.done(),)
            A.wait(PE.done(), *hT_free[p % 2])
            A.do(nc.scalar.copy, hT[p % 2], bank[3][:, 0:IC * PAIR].rearrange("p (j t) -> p j t", j=IC))
            flipped[p] = A.done()
            o["flipped"] = (A.done(),)

        def down(p):
            s = p % 2
            PE.wait(flipped[p], wload[2 * p, "down"], wload[2 * p + 1, "down"], *o["y"])
            for j in range(IC):
                m = P if j < 2 else last
                for half in range(2):
                    mine = slice(half * CAP, (half + 1) * CAP)
                    PE.do(nc.tensor.matmul, bank[4][mine, :], hT[s][0:m, j, mine],
                          ring[(2 * p + half) % 4][2][0:m, j, :], start=j == 0, stop=j == IC - 1)
            hT_free[s] = (PE.done(),)
            for half in range(2):
                e = 2 * p + half
                down_free[e % 4] = (PE.done(),)
                if e + 4 < E:
                    load_down(e + 4)
                mine = slice(half * CAP, (half + 1) * CAP)
                A.wait(PE.done(), *ye_free[half])
                A.do(nc.scalar.activation, ye[half][0:CAP, :], bank[4][mine, :], ACT.Copy,
                     scale=wts[mine, p:p + 1])
                o["y"] = (A.done(),)
                G.wait(A.done(), *o["sum"])
                mark = G.dma(nc.gpsimd.indirect_dma_start, self.slot("ff_sum"), out=y_dram[:, :],
                             out_offset=bass.IndirectOffsetOnAxis(ap=ids1[0:CAP, e:e + 1], axis=0),
                             in_=ye[half][0:CAP, :], in_offset=None, bounds_check=T + CAP - 1,
                             oob_is_err=True, compute_op=ALU.add)
                self.open.append(mark)
                ye_free[half] = (mark,)
                o["sum"] = (mark,)

        gather(0)
        gather(1)
        for e in range(2, 4):
            load_up(e)
            load_down(e)
        spend(2)
        turn(0)
        gather(2)
        left = len(units)
        for p in range(NPAIR + 1):
            if p < NPAIR:
                up(p)
            if p > 0:
                down(p - 1)
            if p < NPAIR:
                flip(p)
                spend(len(units) - left * (NPAIR - 1 - p) // NPAIR)
                if p + 1 < NPAIR:
                    turn(p + 1)
                if p + 3 < NPAIR:
                    gather(p + 3)
        shared_store()
        self.stage_end()
        sb.at = start


    def attention(self, a_dram, y_dram, out_dram):
        nc, d = self.nc, self.d
        PE, V, A, G, SP = self.lanes
        sb, bank = self.sb, self.bank
        start = sb.at
        SCALE = float(1.0 / np.sqrt(np.float32(HEAD)))
        KV = KV_HEADS * HEAD
        C = KV_HEADS
        R = HEADS // C
        COLS = P * QT * (QT + 1) // 2
        offset = [P * t * (t + 1) // 2 for t in range(QT)]
        turned_at = [sum((QT - i) * P for i in range(j)) for j in range(QT)]
        NXA = 3
        wq, wk, wv = sb.cut([HC, H]), sb.cut([HC, KV]), sb.cut([HC, KV])
        wo = sb.cut([HC, H])
        bq, bk = sb.cut([HC]), sb.cut([1])
        bv, bo = sb.cut([KV]), sb.cut([H])
        rope = sb.cut([SEQ])
        mask = sb.cut([SEQ])
        xa = [sb.cut([QT, H]) for _ in range(NXA)]
        xy = sb.cut([QT, H])
        xn = sb.cut([QT, H])
        xnT = xy
        qT = [sb.cut([R, SEQ]) for _ in range(2)]
        kT = [sb.cut([SEQ]) for _ in range(2)]
        vv = [sb.cut([QT, KV]) for _ in range(2)]
        NSC = 6
        sc = [sb.cut([SEQ]) for _ in range(NSC)]
        pr = [sb.cut([C, COLS]) for _ in range(2)]
        prT = sb.cut([C, COLS])
        nb = sb.cut([2, C])
        den = sb.cut([2, C])
        rden = sb.cut([2, C])
        yT = sb.cut([R, SEQ])
        work = self.norm_work(QT)

        for out, in_ in ((wq, d["wqT"].rearrange("(c p) n -> p c n", p=P)),
                         (wk, d["wkT"].rearrange("(c p) n -> p c n", p=P)),
                         (wv, d["wvT"].rearrange("(c p) n -> p c n", p=P)),
                         (wo, d["woT"].rearrange("(c p) n -> p c n", p=P)),
                         (bq, d["bq"]), (bk, d["bk"]),
                         (bv, d["bv"].partition_broadcast(P)),
                         (bo, d["bo"].partition_broadcast(P)),
                         (rope, d["rope"])):
            w_in = self.load("at_w", out, in_)
        G.do(nc.gpsimd.memset, mask, 0.0)
        G.wait(G.done())
        G.do(nc.gpsimd.affine_select, out=mask[:, SEQ - P:], in_=mask[:, SEQ - P:], compare_op=ALU.is_ge,
             fill=NEG, base=0, pattern=[[-1, P]], channel_multiplier=1)
        for lane in (PE, V, A):
            lane.wait(w_in, G.done())

        a_v = a_dram.rearrange("(n p) h -> p n h", p=P)
        y_v = y_dram[0:T, :].rearrange("(n p) h -> p n h", p=P)
        o_v = out_dram.rearrange("(n p) h -> p n h", p=P)
        got, ready = {}, {}
        xa_free, qk_free = [()] * NXA, [(), ()]
        bank_free = [()] * 8
        st = {"xn": (), "xy": (), "yT": (), "prT": [()] * C}

        def load_x(b):
            SP.wait(*xa_free[b % NXA], *st["xy"])
            one = self.load(f"at_a{b % NXA}", xa[b % NXA], a_v[:, b * QT:(b + 1) * QT, :])
            got[b] = (one, self.load("at_y", xy, y_v[:, b * QT:(b + 1) * QT, :]))

        def project(b):
            s, x = b % 2, xa[b % NXA]
            V.wait(*got[b])
            V.do(nc.vector.tensor_tensor, out=x, in0=x, in1=xy, op=ALU.add)
            summed = V.done()
            yield
            normed = self.layernorm(x, xn, work, [summed], st["xn"])
            G.wait(normed)
            G.do(nc.gpsimd.tensor_tensor, out=x, in0=x, in1=over(bo, 1, QT), op=ALU.add)
            biased = G.done()
            yield
            A.wait(summed, *st["xy"])
            for c in range(HC):
                PE.wait(normed, *bank_free[7])
                for t in range(QT):
                    PE.do(nc.tensor.transpose, bank[7][:, t * P:(t + 1) * P], xn[:, t, c * P:(c + 1) * P],
                          self.ident)
                st["xn"] = (PE.done(),)
                A.wait(PE.done())
                A.do(nc.scalar.copy, xnT[:, c, :], bank[7][:, :])
                turned = A.done()
                bank_free[7] = (turned,)
                yield
            V.wait(*qk_free[s])
            for r in range(R + 1):
                PE.wait(turned, *bank_free[7])
                for c in range(HC):
                    w = wq[:, c, r * P:(r + 1) * P] if r < R else wk[:, c, :]
                    PE.do(nc.tensor.matmul, bank[7][:, :], w, xnT[:, c, :], start=c == 0, stop=c == HC - 1)
                V.wait(PE.done())
                V.do(nc.vector.scalar_tensor_tensor, out=qT[s][:, r, :] if r < R else kT[s],
                     in0=bank[7][:, :], scalar=bq[:, r:r + 1] if r < R else bk[:, 0:1], in1=rope,
                     op0=ALU.add, op1=ALU.mult)
                bank_free[7] = (V.done(),)
                yield
            PE.wait(*bank_free[7])
            for t in range(QT):
                for c in range(HC):
                    PE.do(nc.tensor.matmul, bank[7][:, t * P:(t + 1) * P], xnT[:, c, t * P:(t + 1) * P],
                          wv[:, c, :], start=c == 0, stop=c == HC - 1)
            st["xy"] = (PE.done(),)
            V.wait(PE.done())
            V.do(nc.vector.tensor_tensor, out=vv[s], in0=bank[7][:, :].rearrange("p (t k) -> p t k", t=QT),
                 in1=over(bv, 1, QT), op=ALU.add)
            bank_free[7] = (V.done(),)
            ready[b] = (V.done(), biased)
            yield

        quads = [(b, r) for b in range(BATCH) for r in range(R)]
        steps = [(n, t) for n in range(len(quads)) for t in reversed(range(QT))]
        scaled, flipped, evacuated, exped_at = {}, {}, {}, []

        def score(k):
            n, t = steps[k]
            b, r = quads[n]
            s = b % 2
            width = (t + 1) * P
            for c in range(C):
                rows = slice(c * HEAD, (c + 1) * HEAD)
                PE.wait(*ready[b], *bank_free[c])
                PE.do(nc.tensor.matmul, bank[c][:, 0:width], qT[s][rows, r, t * P:(t + 1) * P],
                      kT[s][rows, 0:width], start=True, stop=True)
                scored = PE.done()
                V.wait(scored)
                if len(exped_at) >= NSC:
                    V.wait(exped_at[-NSC])
                i = len(exped_at) % NSC
                V.do(nc.vector.tensor_tensor_reduce, out=sc[i][:, 0:width], in0=bank[c][:, 0:width],
                     in1=mask[:, SEQ - width:], scale=-SCALE, scalar=3e38, op0=ALU.add, op1=ALU.min,
                     accum_out=nb[:, k % 2, c:c + 1])
                bank_free[c] = (V.done(),)
                A.wait(V.done())
                if n >= 2:
                    A.wait(flipped[n - 2, c])
                if k >= 2:
                    A.wait(scaled[k - 2])
                A.do(nc.scalar.activation, pr[n % 2][:, c, offset[t]:offset[t] + width], sc[i][:, 0:width],
                     ACT.Exp, scale=-1.0, bias=nb[:, k % 2, c:c + 1], accum_out=den[:, k % 2, c:c + 1])
                exped_at.append(A.done())
                yield

        def divide(k):
            n, t = steps[k]
            width = (t + 1) * P
            V.wait(exped_at[k * C + C - 1])
            if k >= 2:
                V.wait(scaled[k - 2])
            V.do(nc.vector.reciprocal, rden[:, k % 2, :], den[:, k % 2, :])
            G.wait(V.done())
            own = pr[n % 2][:, :, offset[t]:offset[t] + width]
            G.do(nc.gpsimd.tensor_tensor, out=own, in0=own, in1=over(rden[:, k % 2, :], 2, width), op=ALU.mult)
            scaled[k] = G.done()

        def flip(n, c):
            PE.wait(scaled[n * QT + QT - 1])
            for j, (blocks, lane) in enumerate((((0,), A), ((1,), V), ((2, 3), A))):
                i = 4 + self.flips % 2
                self.flips += 1
                PE.wait(*bank_free[i])
                first = turned_at[blocks[0]]
                width = 0
                for kb in blocks:
                    for t in range(kb, QT):
                        PE.do(nc.tensor.transpose, bank[i][:, width:width + P],
                              pr[n % 2][:, c, offset[t] + kb * P:offset[t] + (kb + 1) * P], self.ident)
                        width += P
                lane.wait(PE.done(), *st["prT"][c])
                lane.do(nc.scalar.copy if lane is A else nc.vector.tensor_copy,
                        prT[:, c, first:first + width], bank[i][:, 0:width])
                bank_free[i] = (lane.done(),)
                evacuated[n, c, j] = lane.done()
                if j == 2:
                    flipped[n, c] = PE.done()
                yield

        def weigh(n):
            b, r = quads[n]
            PE.wait(*bank_free[6])
            for c in range(C):
                for j in range(3):
                    PE.wait(evacuated[n, c, j])
            for j in range(QT):
                for c in range(C):
                    PE.do(nc.tensor.matmul, bank[6][c * HEAD:(c + 1) * HEAD, j * P:SEQ],
                          vv[b % 2][:, j, c * HEAD:(c + 1) * HEAD],
                          prT[:, c, turned_at[j]:turned_at[j] + (QT - j) * P], start=j == 0, stop=j == QT - 1)
            st["prT"] = [(PE.done(),)] * C
            A.wait(PE.done(), *st["yT"])
            A.do(nc.scalar.copy, yT[:, r, :], bank[6][:, :])
            bank_free[6] = (A.done(),)

        def finish(b):
            x = xa[b % NXA]
            PE.wait(A.done())
            qk_free[b % 2] = (PE.done(),)
            for t in range(QT):
                PE.wait(*bank_free[7])
                for r in range(R):
                    PE.do(nc.tensor.matmul, bank[7][:, :], yT[:, r, t * P:(t + 1) * P], wo[:, r, :],
                          start=r == 0, stop=r == R - 1)
                V.wait(PE.done())
                V.do(nc.vector.tensor_tensor, out=x[:, t, :], in0=x[:, t, :], in1=bank[7][:, :],
                     op=ALU.add)
                bank_free[7] = (V.done(),)
            st["yT"] = (PE.done(),)
            SP.wait(V.done())
            xa_free[b % NXA] = (self.store(f"at_o{b % NXA}", o_v[:, b * QT:(b + 1) * QT, :], x),)

        self.flips = 0
        load_x(0)
        for _ in project(0):
            pass
        coming = iter(())
        LAG = 5
        for k in range(len(steps) + LAG + 1):
            m = k - LAG - 1
            if m >= 0 and m % QT == QT - 1:
                weigh(m // QT)
            if k < len(steps):
                b = quads[steps[k][0]][0]
                if k % (R * QT) == 1 and b + 1 < BATCH:
                    load_x(b + 1)
                    coming = project(b + 1)
            scores = score(k) if k < len(steps) else iter(())
            flips = flip((k - LAG) // QT, (k - LAG) % QT) if 0 <= k - LAG < len(steps) else iter(())
            for _ in range(C):
                next(flips, None)
                next(scores, None)
            next(coming, None)
            if k < len(steps):
                divide(k)
            if m >= 0 and m % (R * QT) == R * QT - 1:
                finish(m // (R * QT))
        self.stage_end()
        sb.at = start

    def add_up(self, a_dram, y_dram, out_dram):
        nc, V, SP = self.nc, self.V, self.SP
        start = self.sb.at
        N = 4
        a = [self.sb.cut([QT, H]) for _ in range(N)]
        y = [self.sb.cut([QT, H]) for _ in range(N)]
        a_v = a_dram.rearrange("(b p n) h -> b p n h", p=P, n=QT)
        y_v = y_dram[0:T, :].rearrange("(b p n) h -> b p n h", p=P, n=QT)
        o_v = out_dram.rearrange("(b p n) h -> b p n h", p=P, n=QT)
        free, got = [()] * N, {}

        def fetch(b):
            SP.wait(*free[b % N])
            got[b] = (self.load(f"au_a{b % N}", a[b % N], a_v[b]), self.load(f"au_y{b % N}", y[b % N], y_v[b]))

        for b in range(N - 1):
            fetch(b)
        for b in range(BATCH):
            V.wait(*got[b])
            V.do(nc.vector.tensor_tensor, out=a[b % N], in0=a[b % N], in1=y[b % N], op=ALU.add)
            SP.wait(V.done())
            free[b % N] = (self.store(f"au_o{b % N}", o_v[b], a[b % N]),)
            if b + N - 1 < BATCH:
                fetch(b + N - 1)
        self.stage_end()
        self.sb.at = start


def build(nc, dram, stages="SFAFU"):
    with ExitStack() as ctx:
        p = Program(nc, ctx, dram)
        p.constants()
        if "S" in stages:
            p.state_space(dram["x"], dram["x1"])
        if "F" in stages:
            p.feed_forward(dram["x1"], dram["a"], dram["y"])
        if "A" in stages:
            p.attention(dram["a"], dram["y"], dram["x3"])
        if stages.count("F") == 2:
            p.feed_forward(dram["x3"], dram["a2"], dram["y2"])
        if "U" in stages:
            p.add_up(dram["a2"], dram["y2"], dram["out"])
        block = ctx.enter_context(nc.Block())
        PE, V, A, G, SP = p.lanes

        @block.tensor
        def _(eng):
            PE.play(eng)

        @block.vector
        def _(eng):
            V.play(eng)

        @block.scalar
        def _(eng):
            A.play(eng)

        @block.gpsimd
        def _(eng):
            G.play(eng)

        @block.sync
        def _(eng):
            SP.play(eng)


def rope_factor():
    f = np.float32
    inv = f(10000.0) ** (f(-2.0) * np.arange(HEAD // 2, dtype=f) / f(HEAD))
    theta = np.arange(SEQ, dtype=f)[:, None] * inv[None, :]
    both = (np.cos(theta) + np.sin(theta)).astype(f)
    return np.ascontiguousarray(np.tile(np.concatenate([both, both], axis=1).T, (P // HEAD, 1)))


def lay_out(inputs):
    g = {k: np.asarray(v) for k, v in inputs.items()}
    heads = np.arange(HEADS * HEAD).reshape(4, 4, HEAD).transpose(1, 0, 2).ravel()
    c = np.ascontiguousarray
    return {
        "x": c(g["L0_attn_a_x"].reshape(T, H)),
        "wxT": c(g["L0_attn_a_W_x"].T), "wdtT": c(g["L0_attn_a_W_dt"].T), 
        "par": c(np.stack([g["L0_attn_a_b_dt"], g["L0_attn_a_D_param"]], 1).reshape(HC, P, 2).transpose(1, 0, 2)),
        "A_log": c(g["L0_attn_a_A_log"]),
        "wqT": c(g["L0_attn_b_Wq"][heads].T), "bq": c(g["L0_attn_b_bq"][heads].reshape(HC, P).T),
        "wkT": c(g["L0_attn_b_Wk"].T), "bk": c(g["L0_attn_b_bk"].reshape(P, 1)),
        "wvT": c(g["L0_attn_b_Wv"].T), "bv": c(g["L0_attn_b_bv"]),
        "woT": c(g["L0_attn_b_Wo"].T[heads]), "bo": c(g["L0_attn_b_bo"]),
        "gate_wT": c(g["L0_ffn_gate_w"].T),
        "w_gate": c(g["L0_ffn_w_gate"]), "w_up": c(g["L0_ffn_w_up"]), "w_down": c(g["L0_ffn_w_down"]),
        "sw_gate": c(g["L0_ffn_sw_gate"]), "sw_up": c(g["L0_ffn_sw_up"]), "sw_down": c(g["L0_ffn_sw_down"]),
        "rope": rope_factor(),
    }


SCRATCH = {"bc": (BATCH, 2 * NSTATE, SEQ), "x1": (T, H), "x3": (T, H), "a": (T, H), "a2": (T, H),
           "y": (T + CAP, H), "y2": (T + CAP, H), "xn": (T + CAP, H), "tab": (SLOTS, 2)}


def declare(nc, arrays, stages="SFAFU"):
    dram = {n: nc.dram_tensor(f"in_{n}", a.shape, FP32, kind="ExternalInput").ap() for n, a in arrays.items()}
    for n, shape in SCRATCH.items():
        if n not in dram:
            dram[n] = nc.dram_tensor(f"scratch_{n}", shape, FP32).ap()
    dram["out"] = nc.dram_tensor("out", (T, H), FP32, kind="ExternalOutput").ap()
    build(nc, dram, stages)


def kernel(**inputs):
    import concourse.bacc as bacc
    from concourse.bass_utils import run_bass_kernel_spmd

    arrays = lay_out(inputs)
    nc = bacc.Bacc("TRN2", target_bir_lowering=False, num_devices=1)
    declare(nc, arrays)
    r = run_bass_kernel_spmd(nc, [{f"in_{n}": a for n, a in arrays.items()}], core_ids=[0])
    return r.results[0]["out"].reshape(BATCH, SEQ, H)
```

```python
from contextlib import ExitStack

import numpy as np

import concourse.bass as bass
from concourse import mybir

FP32 = mybir.dt.float32
BF16 = mybir.dt.bfloat16
I32 = mybir.dt.int32
ALU = mybir.AluOpType
ACT = mybir.ActivationFunctionType
AXIS_X = mybir.AxisListType.X

P = 128
BATCH, SEQ, H = 8, 512, 512
T = BATCH * SEQ
NT = T // P
QT = SEQ // P
HC = H // P
NSTATE, DT_RANK = 16, 128
HEADS, KV_HEADS, HEAD = 16, 4, 32
E, TOPK, INTER, CAP = 64, 6, 352, 64
SHARED = 2 * INTER
SLOTS = E * CAP
EPS = 1e-5
NEG = -1e30
BANK = 512
ARENA = 52800

BESIDE_SCAN = 7
PIECES = (5, 9)
UNITS = ((1, 0, 1, 1), (1, 1, 1, 2))
FRONT_AT = ((1, 3), (1, 2))
DIRECT = (8, 4)


class Lane:

    def __init__(self, nc, name):
        self.nc, self.name, self.queue, self.waited = nc, name, [], {}
        self.sem, self.count, self.sems = None, 0, 0
        self.last, self.mark = None, None

    def new_count(self, ctx):
        self.sem = ctx.enter_context(self.nc.semaphore(f"{self.name}_{self.sems}"))
        self.count, self.sems = 0, self.sems + 1

    def do(self, method, *args, **kw):
        self.last = [method, args, kw, None]
        self.queue.append(self.last)

    def done(self):
        if self.last[3] is None:
            self.count += 1
            self.last[3] = (self.sem, 1)
            self.mark = (self.sem, self.count)
        return self.mark

    def wait(self, *marks):
        for sem, value in marks:
            if self.waited.get(sem.name, 0) < value:
                self.waited[sem.name] = value
                self.queue.append(["wait", sem, value, None])

    def dma(self, method, slot, *args, **kw):
        slot.count += 16
        self.queue.append([method, args, kw, (slot.sem, 16)])
        return (slot.sem, slot.count)

    def play(self, engine):
        for method, args, kw, inc in self.queue:
            if isinstance(method, str):
                engine.wait_ge(args, kw)
            elif inc is None:
                method(*args, **kw)
            else:
                method(*args, **kw).then_inc(*inc)


class Slot:

    def __init__(self, ctx, nc, name):
        self.sem, self.count = ctx.enter_context(nc.semaphore(name)), 0


class Arena:

    def __init__(self, base):
        self.base, self.at = base, 0

    def cut(self, shape, dt=FP32):
        n = int(np.prod(shape))
        words = n if dt in (FP32, I32) else (n + 1) // 2
        words = (words + 7) // 8 * 8
        assert self.at + words <= ARENA, (self.at, words)
        view = self.base[:, self.at:self.at + words]
        self.at += words
        if dt != FP32:
            view = view.bitcast(dt)
        view = view[:, 0:n]
        if len(shape) == 2:
            view = view.rearrange("p (a b) -> p a b", a=shape[0])
        if len(shape) == 3:
            view = view.rearrange("p (a b c) -> p a b c", a=shape[0], b=shape[1])
        return view


def over(ap, axis, n):
    v = ap.unsqueeze(axis)
    shape = list(v.shape)
    shape[axis] = n
    return v.to_broadcast(shape)


class Program:
    def __init__(self, nc, ctx, dram):
        self.nc, self.ctx, self.d = nc, ctx, dram
        base = ctx.enter_context(nc.sbuf_tensor("arena", [P, ARENA], FP32))
        self.sb = Arena(base)
        self.bank = [ctx.enter_context(nc.psum_tensor(f"bank{i}", [P, BANK], FP32)) for i in range(8)]
        self.PE, self.V, self.A, self.G, self.SP = (Lane(nc, n) for n in ("pe", "dve", "act", "pool", "sp"))
        self.lanes = [self.PE, self.V, self.A, self.G, self.SP]
        for lane in self.lanes:
            lane.new_count(ctx)
        self.slots, self.open = {}, []

    def slot(self, name):
        if name not in self.slots:
            self.slots[name] = Slot(self.ctx, self.nc, name)
        return self.slots[name]

    def load(self, name, out, in_):
        mark = self.SP.dma(self.nc.sync.dma_start, self.slot(name), out, in_)
        self.open.append(mark)
        return mark

    store = load

    def stage_end(self):
        marks = [lane.done() for lane in self.lanes[:4] if lane.last]
        last = {}
        for sem, value in self.open:
            last[sem.name] = (sem, max(value, last.get(sem.name, (sem, 0))[1]))
        self.open = []
        for lane in self.lanes:
            lane.wait(*marks, *last.values())
        for lane in self.lanes[:4]:
            lane.new_count(self.ctx)

    def constants(self):
        nc, G, V = self.nc, self.G, self.V
        self.ident = self.sb.cut([P])
        self.half = self.sb.cut([8])
        G.do(nc.gpsimd.memset, self.ident, 0.0)
        G.do(nc.gpsimd.memset, self.half, -0.5)
        G.wait(G.done())
        G.do(nc.gpsimd.affine_select, out=self.ident, in_=self.ident, compare_op=ALU.not_equal, fill=1.0,
             base=0, pattern=[[-1, P]], channel_multiplier=1)
        self.ready = G.done()
        for lane in (self.PE, V, self.A, self.SP, G):
            lane.wait(self.ready)

    def layernorm_steps(self, x, xn, work, x_ready, xn_free=()):
        nc, V, G = self.nc, self.V, self.G
        n = x.shape[1]
        stats, mv, rstd = work
        V.wait(*x_ready)
        for i in range(n):
            V.do(nc.vector.bn_stats, out=stats[:, i, :], in_=x[:, i, :])
        V.wait(V.done())
        for i in range(n):
            V.do(nc.vector.bn_aggr, out=mv[:, i, :], in_=stats[:, i, :])
        varied = V.done()
        yield
        G.wait(varied)
        G.do(nc.gpsimd.tensor_scalar, rstd, mv[:, :, 1], EPS, None, ALU.add)
        G.wait(G.done())
        G.do(nc.gpsimd.tensor_tensor, out=rstd, in0=rstd, in1=self.half[:, 0:n], op=ALU.pow)
        scaled = G.done()
        yield
        V.wait(scaled, *xn_free)
        for i in range(n):
            V.do(nc.vector.tensor_scalar, xn[:, i, :], x[:, i, :], mv[:, i, 0:1], rstd[:, i:i + 1],
                 ALU.subtract, ALU.mult)
        self.normed = V.done()

    def layernorm(self, *args):
        for _ in self.layernorm_steps(*args):
            pass
        return self.normed

    def norm_work(self, n):
        return self.sb.cut([n, 6]), self.sb.cut([n, 2]), self.sb.cut([n])


    def state_space(self, x_dram, out_dram, ff, done_here):
        nc, d = self.nc, self.d
        PE, V, A, G, SP = self.lanes
        sb, bank = self.sb, self.bank
        start = sb.at
        NG = 2
        GROUPS = NSTATE // NG
        RING = 2
        HB = 4
        wx = sb.cut([HC, DT_RANK + 2 * NSTATE])
        wdt = sb.cut([H])
        par = sb.cut([HC, 2])
        alog = sb.cut([HC, NSTATE])
        diag = sb.cut([HC, P])
        xin = [sb.cut([QT, H]) for _ in range(2)]
        xn = sb.cut([QT, H])
        xnT = [sb.cut([HC, SEQ]) for _ in range(2)]
        dt = [sb.cut([HC, SEQ]) for _ in range(2)]
        dtx = [sb.cut([HC, SEQ]) for _ in range(2)]
        dtr = sb.cut([SEQ])
        bcs = sb.cut([SEQ])
        bb = [sb.cut([NG, SEQ]) for _ in range(RING)]
        cb = [sb.cut([NG, SEQ]) for _ in range(RING)]
        da = [sb.cut([NG, SEQ]) for _ in range(2)]
        hb = [sb.cut([NG, SEQ]) for _ in range(HB)]
        work = self.norm_work(QT)
        x_v = x_dram.rearrange("(n p) h -> p n h", p=P)
        o_v = out_dram.rearrange("(n p) h -> p n h", p=P)
        bc_dram = d["bc"]

        xload, prepared, bcload, ring_free = {}, {}, {}, [()] * RING
        spare_free, nspare = [()] * 8, [0]

        def spare():
            i = 4 + nspare[0] % 2
            nspare[0] += 1
            PE.wait(*spare_free[i])
            return i

        xin_free, xnT_free, dt_free = [(), ()], [(), ()], [(), ()]
        y_free = [()] * QT
        st = {"dtr": (), "bcs": (), "xn": ()}

        def load_x(b):
            SP.wait(*xin_free[b % 2])
            xload[b] = self.load(f"ss_x{b % 2}", xin[b % 2], x_v[:, b * QT:(b + 1) * QT, :])

        load_x(0)
        w_in = [self.load("ss_w", wx, d["wxT"].rearrange("(c p) k -> p c k", p=P)),
                self.load("ss_w", wdt, d["wdtT"]),
                self.load("ss_w", par, d["par"]),
                self.load("ss_w", alog, d["A_log"].rearrange("(c p) n -> p c n", p=P))][-1:]

        def prepare(b):
            s = b % 2
            soft = dtx[s]
            yield from self.layernorm_steps(xin[s], xn, work, [xload[b]], (*st["xn"], *ff.xn_free))
            normed = self.normed
            yield
            yield
            A.wait(*xnT_free[s])
            late = []

            def take_products():
                for f in late:
                    f()
                late.clear()

            def turn(c):
                i = spare()
                PE.wait(normed)
                for t in range(QT):
                    PE.do(nc.tensor.transpose, bank[i][:, t * P:(t + 1) * P], xn[:, t, c * P:(c + 1) * P],
                          self.ident)
                made = PE.done()

                def taken():
                    A.wait(made)
                    A.do(nc.scalar.copy, xnT[s][:, c, :], bank[i][:, :])
                    spare_free[i] = (A.done(),)
                late.append(taken)

            for c in range(HC):
                take_products()
                turn(c)
                yield
            st["xn"] = (PE.done(),)
            take_products()
            turned = A.done()
            yield

            def project(n, cols, free, out, mark):
                i = spare()
                PE.wait(turned, *w_in)
                for c in range(HC):
                    PE.do(nc.tensor.matmul, bank[i][0:n, :], wx[:, c, cols], xnT[s][:, c, :],
                          start=c == 0, stop=c == HC - 1)
                made = PE.done()

                def taken():
                    A.wait(made, *st[free])
                    A.do(nc.scalar.copy, out, bank[i][0:n, :])
                    spare_free[i] = st[mark] = (A.done(),)
                late.append(taken)

            R = 2 * NSTATE
            project(R, slice(DT_RANK, DT_RANK + R), "bcs", bcs[0:R, :], "bcs_made")
            yield
            take_products()
            SP.wait(*st["bcs_made"])
            stored = self.store("ss_bc", bc_dram[b, :, :], bcs[0:R, :])
            st["bcs"] = (stored,)
            prepared[b] = [stored]
            project(DT_RANK, slice(0, DT_RANK), "dtr", dtr, "dtr_made")
            yield
            take_products()
            yield

            def dt_in(c):
                i = spare()
                PE.wait(*st["dtr_made"])
                PE.do(nc.tensor.matmul, bank[i][:, :], wdt[:, c * P:(c + 1) * P], dtr, start=True, stop=True)
                made = PE.done()

                def taken():
                    A.wait(made)
                    A.do(nc.scalar.activation, soft[:, c, :], bank[i][:, :], ACT.Abs, bias=par[:, c, 0:1])
                    A.do(nc.scalar.activation, dt[s][:, c, :], bank[i][:, :], ACT.Relu, bias=par[:, c, 0:1])
                    spare_free[i] = (A.done(),)
                late.append(taken)

            A.wait(*dt_free[s], *w_in)
            for c in range(HC):
                take_products()
                dt_in(c)
                yield
            st["dtr"] = (PE.done(),)
            take_products()
            yield
            A.wait(A.done())
            for half in (slice(0, HC // 2), slice(HC // 2, HC)):
                A.do(nc.scalar.activation, soft[:, half, :], soft[:, half, :], ACT.Exp, scale=-1.0)
                exped = A.done()
                yield
            A.wait(exped)
            logged = []
            for half in (slice(0, HC // 2), slice(HC // 2, HC)):
                A.do(nc.scalar.activation, soft[:, half, :], soft[:, half, :], ACT.Ln, bias=1.0)
                logged.append(A.done())
                yield
            for half, mark in zip((slice(0, HC // 2), slice(HC // 2, HC)), logged):
                V.wait(mark)
                V.do(nc.vector.tensor_tensor, out=dt[s][:, half, :], in0=dt[s][:, half, :], in1=soft[:, half, :],
                     op=ALU.add)
                summed_dt = V.done()
                yield
                G.wait(summed_dt)
                G.do(nc.gpsimd.tensor_tensor, out=dtx[s][:, half, :], in0=dt[s][:, half, :],
                     in1=xnT[s][:, half, :], op=ALU.mult)
            prepared[b].append(G.done())
            yield

        def load_bc(n):
            b, g = divmod(n, GROUPS)
            r = n % RING
            SP.wait(prepared[b][0], *ring_free[r])
            for buf, row, name in ((bb, 0, "b"), (cb, NSTATE, "c")):
                src = bc_dram[b, row + g * NG:row + (g + 1) * NG, :].partition_broadcast(P)
                bcload[b, g, name] = self.load(f"ss_{name}{r}", buf[r], src)

        def go_on(q):
            ff.xn_free += st["xn"]
            front = ff.front(q, xin[q % 2], xn, xin_done[q], spare, give_bank, fine=True)
            for _ in range(2):
                next(front)
                yield
            next(front)
            xin_free[q % 2] = ff.x_read + ff.x_stored[q]
            if q + 2 < BATCH:
                load_x(q + 2)
            yield
            yield from front

        def give_bank(i, mark):
            spare_free[i] = (mark,)

        def finish(b, summed):
            nonlocal beside
            s = b % 2
            V.wait(summed)
            for t in range(QT):
                V.do(nc.vector.tensor_tensor, out=xin[s][:, t, :], in0=xin[s][:, t, :], in1=bank[t][:, :],
                     op=ALU.add)
                y_free[t] = (V.done(),)
            xin_done[b] = (V.done(),)
            SP.wait(V.done())
            ff.x_stored[b] = (self.store(f"ss_out{s}", o_v[:, b * QT:(b + 1) * QT, :], xin[s]),)
            if b < done_here:
                while (ff.shared_up, b - 2, ff.SC - 1) in ff.units:
                    next(pieces)
                ff.end_piece()
                ff.xnT_free[b] = (PE.done(),)
                beside = go_on(b)
            else:
                xin_free[s] = ff.x_stored[b]
                if b + 2 < BATCH:
                    load_x(b + 2)

        for _ in prepare(0):
            pass
        load_x(1)
        ff.load_weights()
        for lane in (PE, V, A, G):
            lane.wait(*w_in)
        A.do(nc.scalar.activation, alog, alog, ACT.Exp)
        V.wait(A.done())
        V.do(nc.vector.tensor_scalar, alog, alog, -1.0, None, ALU.mult)
        for t in da:
            V.do(nc.vector.memset, t[:, :, 0:1], 0.0)
        for c in range(HC):
            V.do(nc.vector.tensor_scalar, diag[:, c, :], self.ident, par[:, c, 1:2], None, ALU.mult)
        A.wait(V.done())
        PE.wait(V.done())
        xin_done, beside = {}, iter(())
        pieces = ff.run_units()
        next_bc = 0
        steps = [(b, g, c) for b in range(BATCH) for g in range(GROUPS) for c in range(HC)]
        scanned, summed, multiplied = {}, {}, {}
        coming = iter(())
        for k in range(len(steps) + 1):
            if k < len(steps):
                b, g, c = steps[k]
                s, r = b % 2, (b * GROUPS + g) % RING
                if c == 1 or k == 0:
                    while (next_bc < min(BATCH * GROUPS, b * GROUPS + g + RING)
                           and next_bc // GROUPS in prepared):
                        load_bc(next_bc)
                        next_bc += 1
                if g == 0 and c == 0:
                    A.wait(prepared[b][1])
                    G.wait(prepared[b][1])
                if k >= 2:
                    A.wait(scanned[k - 2])
                for n in range(NG):
                    A.do(nc.scalar.activation, da[k % 2][:, n, 1:SEQ], dt[s][:, c, 1:SEQ], ACT.Exp,
                         scale=alog[:, c, g * NG + n:g * NG + n + 1])
                decay = A.done()
                G.wait(bcload[b, g, "b"])
                if k >= HB:
                    G.wait(summed[k - HB])
                G.do(nc.gpsimd.tensor_tensor, out=hb[k % HB], in0=over(dtx[s][:, c, :], 1, NG), in1=bb[r],
                     op=ALU.mult)
                inflow = G.done()
                if g == GROUPS - 1 and c == HC - 1:
                    dt_free[s] = (decay, inflow)
                V.wait(decay, inflow)
                flat = "p a b -> p (a b)"
                V.do(nc.vector.tensor_tensor_scan, out=hb[k % HB].rearrange(flat), data0=da[k % 2].rearrange(flat),
                     data1=hb[k % HB].rearrange(flat), initial=0.0, op0=ALU.mult, op1=ALU.add)
                scanned[k] = V.done()
                if b > 0 and g == 0 and c == 1:
                    finish(b - 1, summed[k - 2])
            if k > 0:
                next(coming, None)
                if next(beside, "over") == "over" and k * PIECES[0] % PIECES[1] < PIECES[0]:
                    next(pieces)
                b, g, c = steps[k - 1]
                s, r = b % 2, (b * GROUPS + g) % RING
                V.wait(scanned[k - 1], bcload[b, g, "c"])
                w = hb[(k - 1) % HB]
                V.do(nc.vector.tensor_tensor, out=w, in0=w, in1=cb[r], op=ALU.mult)
                multiplied[k - 1] = V.done()
                chan = slice(c * P, (c + 1) * P)
                first = g == 0 and c == 0
                for t in range(QT):
                    toks = slice(t * P, (t + 1) * P)
                    if first:
                        PE.wait(*y_free[t])
                    if g == 0:
                        PE.do(nc.tensor.matmul, bank[t][:, chan], xnT[s][:, c, toks], diag[:, c, :],
                              start=first, stop=False, skip_group_check=True)
                PE.wait(multiplied[k - 1])
                for n in range(NG):
                    for t in range(QT):
                        PE.do(nc.tensor.matmul, bank[t][:, chan], w[:, n, t * P:(t + 1) * P], self.ident,
                              is_transpose=True, start=False,
                              stop=g == GROUPS - 1 and n == NG - 1, skip_group_check=True)
                summed[k - 1] = PE.done()
                if c == HC - 1:
                    ring_free[r] = (multiplied[k - 1], inflow)
                    if g == 0:
                        xnT_free[s] = (summed[k - 1],)
                        if b + 1 < BATCH:
                            coming = prepare(b + 1)
                if g == GROUPS - 1 and c == HC - 1 and k == len(steps):
                    finish(b, summed[k - 1])
        ff.end_piece()
        ff.take_products()
        self.stage_end()
        sb.at = start


    def attention(self, x_dram, out_dram):
        nc, d = self.nc, self.d
        PE, V, A, G, SP = self.lanes
        sb, bank = self.sb, self.bank
        start = sb.at
        SCALE = float(1.0 / np.sqrt(np.float32(HEAD)))
        KV = KV_HEADS * HEAD
        C = KV_HEADS
        R = HEADS // C
        COLS = P * QT * (QT + 1) // 2
        offset = [P * t * (t + 1) // 2 for t in range(QT)]
        turned_at = [sum((QT - i) * P for i in range(j)) for j in range(QT)]
        NXA = 3
        wq, wk, wv = sb.cut([HC, H]), sb.cut([HC, KV]), sb.cut([HC, KV])
        wo = sb.cut([HC, H])
        bq, bk = sb.cut([HC]), sb.cut([1])
        bv, bo = sb.cut([KV]), sb.cut([H])
        rope = sb.cut([SEQ])
        mask = sb.cut([SEQ])
        xa = [sb.cut([QT, H]) for _ in range(NXA)]
        xn = sb.cut([QT, H])
        xnT = sb.cut([HC, SEQ])
        qT = [sb.cut([R, SEQ]) for _ in range(2)]
        kT = [sb.cut([SEQ]) for _ in range(2)]
        vv = [sb.cut([QT, KV]) for _ in range(2)]
        NSC = 6
        sc = [sb.cut([SEQ]) for _ in range(NSC)]
        pr = [sb.cut([C, COLS]) for _ in range(2)]
        prT = sb.cut([C, COLS])
        nb = sb.cut([2, C])
        den = sb.cut([2, C])
        rden = sb.cut([2, C])
        yT = sb.cut([R, SEQ])
        work = self.norm_work(QT)

        G.do(nc.gpsimd.memset, mask, 0.0)
        G.wait(G.done())
        G.do(nc.gpsimd.affine_select, out=mask[:, SEQ - P:], in_=mask[:, SEQ - P:], compare_op=ALU.is_ge,
             fill=NEG, base=0, pattern=[[-1, P]], channel_multiplier=1)
        V.wait(G.done())

        x_v = x_dram[0:T, :].rearrange("(n p) h -> p n h", p=P)
        o_v = out_dram.rearrange("(n p) h -> p n h", p=P)
        got, ready = {}, {}
        xa_free, qk_free = [()] * NXA, [(), ()]
        bank_free = [()] * 8
        st = {"xn": (), "xnT": (), "yT": (), "prT": [()] * C}

        def load_x(b):
            SP.wait(*xa_free[b % NXA])
            got[b] = self.load(f"at_x{b % NXA}", xa[b % NXA], x_v[:, b * QT:(b + 1) * QT, :])

        def project(b):
            s, x = b % 2, xa[b % NXA]
            yield from self.layernorm_steps(x, xn, work, [got[b]], st["xn"])
            normed = self.normed
            G.wait(normed, w_in)
            G.do(nc.gpsimd.tensor_tensor, out=x, in0=x, in1=over(bo, 1, QT), op=ALU.add)
            biased = G.done()
            yield
            A.wait(*st["xnT"])
            for c in range(HC):
                PE.wait(normed, *bank_free[7])
                for t in range(QT):
                    PE.do(nc.tensor.transpose, bank[7][:, t * P:(t + 1) * P], xn[:, t, c * P:(c + 1) * P],
                          self.ident)
                st["xn"] = (PE.done(),)
                A.wait(PE.done())
                A.do(nc.scalar.copy, xnT[:, c, :], bank[7][:, :])
                turned = A.done()
                bank_free[7] = (turned,)
                yield
            PE.wait(w_in)
            V.wait(w_in, *qk_free[s])
            for r in range(R + 1):
                PE.wait(turned, *bank_free[7])
                for c in range(HC):
                    w = wq[:, c, r * P:(r + 1) * P] if r < R else wk[:, c, :]
                    PE.do(nc.tensor.matmul, bank[7][:, :], w, xnT[:, c, :], start=c == 0, stop=c == HC - 1)
                V.wait(PE.done())
                V.do(nc.vector.scalar_tensor_tensor, out=qT[s][:, r, :] if r < R else kT[s],
                     in0=bank[7][:, :], scalar=bq[:, r:r + 1] if r < R else bk[:, 0:1], in1=rope,
                     op0=ALU.add, op1=ALU.mult)
                bank_free[7] = (V.done(),)
                yield
            PE.wait(*bank_free[7])
            for t in range(QT):
                for c in range(HC):
                    PE.do(nc.tensor.matmul, bank[7][:, t * P:(t + 1) * P], xnT[:, c, t * P:(t + 1) * P],
                          wv[:, c, :], start=c == 0, stop=c == HC - 1)
            st["xnT"] = (PE.done(),)
            V.wait(PE.done())
            V.do(nc.vector.tensor_tensor, out=vv[s], in0=bank[7][:, :].rearrange("p (t k) -> p t k", t=QT),
                 in1=over(bv, 1, QT), op=ALU.add)
            bank_free[7] = (V.done(),)
            ready[b] = (V.done(), biased)
            yield

        quads = [(b, r) for b in range(BATCH) for r in range(R)]
        steps = [(n, t) for n in range(len(quads)) for t in reversed(range(QT))]
        scaled, flipped, evacuated, exped_at = {}, {}, {}, []

        def score(k):
            n, t = steps[k]
            b, r = quads[n]
            s = b % 2
            width = (t + 1) * P
            for c in range(C):
                rows = slice(c * HEAD, (c + 1) * HEAD)
                PE.wait(*ready[b], *bank_free[c])
                PE.do(nc.tensor.matmul, bank[c][:, 0:width], qT[s][rows, r, t * P:(t + 1) * P],
                      kT[s][rows, 0:width], start=True, stop=True)
                scored = PE.done()
                V.wait(scored)
                if len(exped_at) >= NSC:
                    V.wait(exped_at[-NSC])
                i = len(exped_at) % NSC
                V.do(nc.vector.tensor_tensor_reduce, out=sc[i][:, 0:width], in0=bank[c][:, 0:width],
                     in1=mask[:, SEQ - width:], scale=-SCALE, scalar=3e38, op0=ALU.add, op1=ALU.min,
                     accum_out=nb[:, k % 2, c:c + 1])
                bank_free[c] = (V.done(),)
                A.wait(V.done())
                if n >= 2:
                    A.wait(flipped[n - 2, c])
                if k >= 2:
                    A.wait(scaled[k - 2])
                A.do(nc.scalar.activation, pr[n % 2][:, c, offset[t]:offset[t] + width], sc[i][:, 0:width],
                     ACT.Exp, scale=-1.0, bias=nb[:, k % 2, c:c + 1], accum_out=den[:, k % 2, c:c + 1])
                exped_at.append(A.done())
                yield

        def divide(k):
            n, t = steps[k]
            width = (t + 1) * P
            V.wait(exped_at[k * C + C - 1])
            if k >= 2:
                V.wait(scaled[k - 2])
            V.do(nc.vector.reciprocal, rden[:, k % 2, :], den[:, k % 2, :])
            G.wait(V.done())
            own = pr[n % 2][:, :, offset[t]:offset[t] + width]
            G.do(nc.gpsimd.tensor_tensor, out=own, in0=own, in1=over(rden[:, k % 2, :], 2, width), op=ALU.mult)
            scaled[k] = G.done()

        def flip(n, c):
            PE.wait(scaled[n * QT + QT - 1])
            for j, (blocks, lane) in enumerate((((0,), A), ((1,), V), ((2, 3), A))):
                i = 4 + self.flips % 2
                self.flips += 1
                PE.wait(*bank_free[i])
                first = turned_at[blocks[0]]
                width = 0
                for kb in blocks:
                    for t in range(kb, QT):
                        PE.do(nc.tensor.transpose, bank[i][:, width:width + P],
                              pr[n % 2][:, c, offset[t] + kb * P:offset[t] + (kb + 1) * P], self.ident)
                        width += P
                lane.wait(PE.done(), *st["prT"][c])
                lane.do(nc.scalar.copy if lane is A else nc.vector.tensor_copy,
                        prT[:, c, first:first + width], bank[i][:, 0:width])
                bank_free[i] = (lane.done(),)
                evacuated[n, c, j] = lane.done()
                if j == 2:
                    flipped[n, c] = PE.done()
                yield

        def weigh(n):
            b, r = quads[n]
            PE.wait(*bank_free[6])
            for c in range(C):
                for j in range(3):
                    PE.wait(evacuated[n, c, j])
            for j in range(QT):
                for c in range(C):
                    PE.do(nc.tensor.matmul, bank[6][c * HEAD:(c + 1) * HEAD, j * P:SEQ],
                          vv[b % 2][:, j, c * HEAD:(c + 1) * HEAD],
                          prT[:, c, turned_at[j]:turned_at[j] + (QT - j) * P], start=j == 0, stop=j == QT - 1)
            st["prT"] = [(PE.done(),)] * C
            A.wait(PE.done(), *st["yT"])
            A.do(nc.scalar.copy, yT[:, r, :], bank[6][:, :])
            bank_free[6] = (A.done(),)

        def finish(b):
            x = xa[b % NXA]
            PE.wait(A.done())
            qk_free[b % 2] = (PE.done(),)
            for t in range(QT):
                PE.wait(*bank_free[7])
                for r in range(R):
                    PE.do(nc.tensor.matmul, bank[7][:, :], yT[:, r, t * P:(t + 1) * P], wo[:, r, :],
                          start=r == 0, stop=r == R - 1)
                V.wait(PE.done())
                V.do(nc.vector.tensor_tensor, out=x[:, t, :], in0=x[:, t, :], in1=bank[7][:, :],
                     op=ALU.add)
                bank_free[7] = (V.done(),)
            st["yT"] = (PE.done(),)
            SP.wait(V.done())
            xa_free[b % NXA] = (self.store(f"at_o{b % NXA}", o_v[:, b * QT:(b + 1) * QT, :], x),)

        self.flips = 0
        load_x(0)
        for out, in_ in ((wq, d["wqT"].rearrange("(c p) n -> p c n", p=P)),
                         (wk, d["wkT"].rearrange("(c p) n -> p c n", p=P)),
                         (wv, d["wvT"].rearrange("(c p) n -> p c n", p=P)),
                         (wo, d["woT"].rearrange("(c p) n -> p c n", p=P)),
                         (bq, d["bq"]), (bk, d["bk"]),
                         (bv, d["bv"].partition_broadcast(P)),
                         (bo, d["bo"].partition_broadcast(P)),
                         (rope, d["rope"])):
            w_in = self.load("at_w", out, in_)
        for _ in project(0):
            pass
        coming = iter(())
        LAG = 5
        for k in range(len(steps) + LAG + 1):
            m = k - LAG - 1
            if m >= 0 and m % QT == QT - 1:
                weigh(m // QT)
            if k < len(steps):
                b = quads[steps[k][0]][0]
                if k % (R * QT) == 1 and b + 1 < BATCH:
                    load_x(b + 1)
                    coming = project(b + 1)
            scores = score(k) if k < len(steps) else iter(())
            flips = flip((k - LAG) // QT, (k - LAG) % QT) if 0 <= k - LAG < len(steps) else iter(())
            next(coming, None)
            for c in range(C):
                next(flips, None)
                next(scores, None)
                if c == 0 and 0 < k <= len(steps):
                    divide(k - 1)
            if m >= 0 and m % (R * QT) == R * QT - 1:
                finish(m // (R * QT))
        self.stage_end()
        sb.at = start


class FeedForward:

    NQ = T // BANK
    SC = (SHARED + P - 1) // P
    LAST_S = SHARED - (SC - 1) * P
    OUT = 3

    def __init__(self, prog, x_dram, y_dram, banks, direct, nlogits):
        self.p, self.x_dram, self.y_dram, self.direct = prog, x_dram, y_dram, direct
        nc, sb, d = prog.nc, prog.sb, prog.d
        self.start = sb.at
        assert self.LAST_S == P // 2
        self.n_v = d["xn"][0:T, :].rearrange("(n p) h -> p n h", p=P)
        self.y_v = y_dram[0:T, :].rearrange("(n p) h -> p n h", p=P)
        self.gw = sb.cut([HC, E])
        self.logits = [sb.cut([QT, E]) for _ in range(nlogits)]
        self.swg, self.swu = sb.cut([HC, SHARED]), sb.cut([HC, SHARED])
        self.swd = sb.cut([self.SC, H])
        self.shT = sb.cut([self.SC, BANK])
        self.ssg = sb.cut([BANK])
        self.so = [sb.cut([H]) for _ in range(self.OUT)]
        self.token_ids = sb.cut([NT], I32)
        self.logits_free = [()] * nlogits
        self.work = prog.norm_work(QT)
        self.xn_free = ()
        self.xnT = {}
        self.xnT_free = {}
        self.piece = ()
        self.x_stored = [()] * self.NQ
        self.copied, self.quad_ready, self.logged = {}, {}, {}
        self.late = None
        self.take_banks(*banks)
        self.h_made, self.h_free, self.ssg_free = (), (), ()
        self.so_free, self.fetched, self.sums = [()] * self.OUT, {}, []
        self.summing = ()
        self.units = [(f, q, k) for q in range(self.NQ)
                      for f, n in ((self.shared_up, self.SC), (self.shared_down, QT)) for k in range(n)]
        self.units.reverse()
        prog.G.do(nc.gpsimd.iota, self.token_ids, pattern=[[P, NT]], base=0, channel_multiplier=1)
        self.listed = prog.G.done()

    def take_banks(self, gate, up, out):
        self.take_products()
        self.gate, self.up, self.out = gate, up, out
        self.bank_free = {i: () for i in (gate, up, out)}

    def keep_all(self):
        for q in range(self.NQ):
            self.xnT[q] = self.p.sb.cut([HC, BANK])

    def load_weights(self):
        p, d = self.p, self.p.d
        self.gw_in = p.load("ff_gw", self.gw, d["gate_wT"].rearrange("(p c) e -> p c e", c=HC))
        p.load("ff_sw", self.swg, d["sw_gate"].rearrange("(p c) i -> p c i", c=HC))
        p.load("ff_sw", self.swu, d["sw_up"].rearrange("(p c) i -> p c i", c=HC))
        p.load("ff_sw", self.swd[:, 0:self.SC - 1, :],
               d["sw_down"][0:(self.SC - 1) * P, :].rearrange("(j p) h -> p j h", p=P))
        self.sw_in = p.load("ff_sw", self.swd[P - self.LAST_S:, self.SC - 1, :], d["sw_down"][(self.SC - 1) * P:, :])

    def front(self, q, x, xn, x_ready, take_bank, give_bank, fine=False):
        p, nc = self.p, self.p.nc
        PE, V, A, SP = p.PE, p.V, p.A, p.SP
        steps = p.layernorm_steps(x, xn, self.work, x_ready, self.xn_free)
        if fine:
            yield from steps
        else:
            for _ in steps:
                pass
        normed = p.normed
        if q < self.direct:
            self.copied[q] = ()
        else:
            SP.wait(*x_ready)
            self.copied[q] = (p.store(f"ff_y{q % 2}", self.y_v[:, q * QT:(q + 1) * QT, :], x),)
        self.x_read = (normed,) + self.copied[q]
        SP.wait(normed)
        stored = p.store("ff_n", self.n_v[:, q * QT:(q + 1) * QT, :], xn)
        yield
        cols = xn.rearrange("p t (m c) -> p t c m", c=HC)
        xnT = self.xnT[q]
        A.wait(*self.xnT_free.get(q, ()))
        for c in range(HC):
            b = take_bank()
            PE.wait(normed)
            for t in range(QT):
                PE.do(nc.tensor.transpose, p.bank[b][:, t * P:(t + 1) * P], cols[:, t, c, :], p.ident)
            A.wait(PE.done())
            A.do(nc.scalar.copy, xnT[:, c, :], p.bank[b][:, :])
            give_bank(b, A.done())
        self.xn_free = (PE.done(), stored)
        self.quad_ready[q] = (A.done(),)
        yield
        b = take_bank()
        PE.wait(self.gw_in, A.done())
        logits = p.bank[b][:, 0:QT * E].rearrange("p (t e) -> p t e", t=QT)
        for t in range(QT):
            for c in range(HC):
                PE.do(nc.tensor.matmul, logits[:, t, :], xnT[:, c, t * P:(t + 1) * P], self.gw[:, c, :],
                      start=c == 0, stop=c == HC - 1)
        i = q % len(self.logits)
        A.wait(PE.done(), *self.logits_free[i])
        A.do(nc.scalar.copy, self.logits[i], logits)
        self.logged[q] = A.done()
        give_bank(b, A.done())
        yield

    def take_products(self):
        late, self.late = self.late, None
        if late:
            late()

    def shared_up(self, q, j):
        p, nc = self.p, self.p.nc
        PE, V, A, bank = p.PE, p.V, p.A, p.bank
        whole = j < self.SC - 1
        m = P if whole else self.LAST_S
        cols = slice(j * P, j * P + m)
        gate_rows = slice(0, m)
        up_rows = slice(P - m, P)
        gate, up = bank[self.gate][gate_rows, :], bank[self.up][up_rows, :]
        gated, hidden = self.ssg[up_rows, :], self.shT[up_rows, j, :]

        def products(*parts):
            for c in range(HC):
                for w, out in parts:
                    PE.do(nc.tensor.matmul, out, w[:, c, cols], self.xnT[q][:, c, :], start=c == 0,
                          stop=c == HC - 1)
            return PE.done()

        def take_gate():
            A.wait(gate_made, *self.ssg_free)
            A.do(nc.scalar.activation, gated, gate, ACT.Silu)
            self.bank_free[self.gate] = (A.done(),)

        def take_up():
            V.wait(*self.bank_free[self.gate], up_made, *self.h_free)
            V.do(nc.vector.tensor_tensor, out=hidden, in0=gated, in1=up, op=ALU.mult)
            self.bank_free[self.up] = self.ssg_free = self.h_made = (V.done(),)

        self.take_products()
        PE.wait(self.sw_in, *self.quad_ready[q], *self.bank_free[self.gate])
        if whole:
            gate_made = products((self.swg, gate))
        else:
            PE.wait(*self.bank_free[self.up])
            gate_made = up_made = products((self.swg, gate), (self.swu, up))
        self.late = take_gate
        yield
        self.take_products()
        if whole:
            PE.wait(*self.bank_free[self.up])
            up_made = products((self.swu, up))
        else:
            self.fetch_x(q * QT)
        self.late = take_up
        yield

    def shared_down(self, q, t):
        p, nc = self.p, self.p.nc
        PE, V, bank = p.PE, p.V, p.bank[self.out]
        i = q * QT + t
        s = i % self.OUT

        def taken():
            if q < self.direct:
                V.wait(made, self.fetched[i])
                V.do(nc.vector.tensor_tensor, out=self.so[s], in0=self.so[s], in1=bank[:, :], op=ALU.add)
            else:
                V.wait(made, *self.so_free[s])
                V.do(nc.vector.tensor_copy, self.so[s], bank[:, :])
            self.bank_free[self.out] = (V.done(),)
            self.sums.append((i, s, V.done()))

        self.queue_sums()
        self.take_products()
        if t < QT - 1:
            self.fetch_x(i + 1)
        PE.wait(*self.h_made, *self.bank_free[self.out])
        for j in range(self.SC):
            rows = slice(0 if j < self.SC - 1 else P - self.LAST_S, P)
            PE.do(nc.tensor.matmul, bank[:, :], self.shT[rows, j, t * P:(t + 1) * P], self.swd[rows, j, :],
                  start=j == 0, stop=j == self.SC - 1)
            if j == self.SC // 2 - 1:
                yield
        if t == QT - 1:
            self.h_free = (PE.done(),)
        made = PE.done()
        self.late = taken
        yield

    def fetch_x(self, i):
        if i < self.direct * QT:
            s = i % self.OUT
            self.p.SP.wait(*self.so_free[s], *self.x_stored[i // QT])
            self.fetched[i] = self.p.load(f"ff_so{s}", self.so[s], self.x_dram[i * P:(i + 1) * P, :])

    def queue_sums(self):
        p = self.p
        for i, s, made in self.sums:
            if i // QT < self.direct:
                p.SP.wait(made)
                self.so_free[s] = (p.store(f"ff_so{s}", self.y_dram[i * P:(i + 1) * P, :], self.so[s]),)
            else:
                p.G.wait(made, *self.copied[i // QT])
                self.so_free[s] = (self.add_rows(self.so[s], self.token_ids[:, i:i + 1]),)
        self.sums = []

    def add_rows(self, rows, row_ids):
        p = self.p
        p.G.wait(*self.summing)
        mark = p.G.dma(p.nc.gpsimd.indirect_dma_start, p.slot("ff_sum"), out=self.y_dram[:, :],
                       out_offset=bass.IndirectOffsetOnAxis(ap=row_ids, axis=0),
                       in_=rows, in_offset=None, bounds_check=T + CAP - 1,
                       oob_is_err=True, compute_op=ALU.add)
        p.open.append(mark)
        self.summing = (mark,)
        return mark

    def spend(self, n):
        while n > 0 and self.units and self.units[-1][1] in self.quad_ready:
            f, q, k = self.units.pop()
            for _ in f(q, k):
                pass
            n -= 1

    def run_units(self):
        while True:
            if self.units and self.units[-1][1] in self.quad_ready:
                f, q, k = self.units.pop()
                self.piece = f(q, k)
                for _ in self.piece:
                    yield
            else:
                yield

    def end_piece(self):
        for _ in self.piece:
            pass

    def rest(self, fronted, early, front_at, nw, nx, ny):
        prog, nc, d = self.p, self.p.nc, self.p.d
        PE, V, A, G, SP = prog.lanes
        sb, bank = prog.sb, prog.bank
        x_dram, y_dram, xn_dram, tab = self.x_dram, self.y_dram, d["xn"], d["tab"]
        x_v = x_dram.rearrange("(n p) h -> p n h", p=P)
        PAIR = 2 * CAP
        NPAIR = E // 2
        NQ = self.NQ
        IC = 3
        last = INTER - 2 * P

        ids = sb.cut([NPAIR], I32)
        wts = sb.cut([NPAIR])
        ids1 = sb.cut([E], I32)
        xe = [sb.cut([H]) for _ in range(nx)]

        def weights():
            return sb.cut([HC, INTER]), sb.cut([HC, INTER]), sb.cut([IC, H])

        AHEAD = nw - 2
        ring = [weights() for _ in range(AHEAD)]
        region = sb.at

        tri = sb.cut([P], BF16)
        ones = sb.cut([P], BF16)
        trif = sb.cut([P])
        token = sb.cut([NT])
        first = sb.cut([E])
        pad = sb.cut([E, 2])
        xt = [sb.cut([QT, H]) for _ in range(2)]
        xn = sb.cut([QT, H])
        score = sb.cut([QT, E + 2])
        marked = sb.cut([QT, E + 2])
        mask = sb.cut([QT, E], BF16)
        seen = sb.cut([E], BF16)
        small = sb.cut([3, QT])
        top = sb.cut([QT, 8])
        six = sb.cut([QT, 8])
        valid = sb.cut([QT, E])
        code = sb.cut([QT, E])
        best = sb.cut([QT, 8])
        where = [sb.cut([QT, 8], I32) for _ in range(2)]
        equal = sb.cut([QT * TOPK, E])
        pair = [sb.cut([QT, TOPK, 2]) for _ in range(2)]
        tab2 = sb.cut([NPAIR, 2])
        tab1 = sb.cut([E, 2])
        zero = sb.cut([H])

        G.do(nc.gpsimd.memset, trif, 1.0)
        G.do(nc.gpsimd.memset, ones, 1.0)
        G.do(nc.gpsimd.memset, seen, 0.0)
        G.do(nc.gpsimd.memset, six, -1.0)
        G.do(nc.gpsimd.memset, score, -1.0)
        G.do(nc.gpsimd.memset, pad, 0.0)
        G.do(nc.gpsimd.memset, zero, 0.0)
        G.do(nc.gpsimd.iota, token, pattern=[[P, NT]], base=0, channel_multiplier=1,
             allow_small_or_imprecise_dtypes=True)
        G.do(nc.gpsimd.iota, first, pattern=[[-CAP, E]], base=SLOTS, channel_multiplier=0,
             allow_small_or_imprecise_dtypes=True)
        G.wait(G.done())
        G.do(nc.gpsimd.affine_select, out=trif, in_=trif, compare_op=ALU.is_gt, fill=0.0, base=0,
             pattern=[[1, P]], channel_multiplier=-1)
        G.do(nc.gpsimd.iota, pad[:, :, 0], pattern=[[0, E]], base=T, channel_multiplier=1,
             allow_small_or_imprecise_dtypes=True)
        G.wait(G.done())
        G.do(nc.gpsimd.tensor_copy, tri, trif)
        set_up = G.done()

        x_free, xload = [(), ()], {}
        front_free = {0: (), 3: ()}

        def load_x(q):
            SP.wait(*x_free[q % 2])
            xload[q] = prog.load(f"ff_x{q % 2}", xt[q % 2], x_v[:, q * QT:(q + 1) * QT, :])

        def take_bank():
            b = next(iter(front_free))
            PE.wait(*front_free.pop(b))
            return b

        def give_bank(b, mark):
            front_free[b] = (mark,)

        for q in range(fronted, min(fronted + 2, NQ)):
            load_x(q)
        if fronted == 0:
            self.load_weights()
        for lane in (PE, V, SP, G):
            lane.wait(set_up, self.listed)
        padded = prog.store("ff_pad", tab.rearrange("(e c) t -> c e t", c=CAP), pad[0:CAP])
        prog.store("ff_pad2", xn_dram[T:T + CAP, :], zero[0:CAP, :])
        prog.store("ff_pad2", y_dram[T:T + CAP, :], zero[0:CAP, :])
        pads = len(prog.open) - 1

        st = {"pos": (), "score": (), "where": [(), ()]}

        def turn_quad(q):
            for _ in self.front(q, xt[q % 2], xn, [xload[q]], take_bank, give_bank):
                x_free[q % 2] = self.x_read
                yield
            if q + 2 < NQ:
                load_x(q + 2)

        def route(q):
            logits = self.logits[q % len(self.logits)]
            V.wait(self.logged[q], *st["score"])
            V.do(nc.vector.tensor_reduce, out=small[:, 0, :], in_=logits, axis=AXIS_X, op=ALU.max)
            V.wait(V.done())
            own = score[:, :, 0:E]
            V.do(nc.vector.tensor_tensor, out=own, in0=logits, in1=over(small[:, 0, :], 2, E), op=ALU.subtract)
            self.logits_free[q % len(self.logits)] = (V.done(),)
            A.wait(V.done())
            A.do(nc.scalar.activation, own, own, ACT.Exp)
            exped = A.done()
            yield
            V.wait(exped)
            V.do(nc.vector.tensor_reduce, out=small[:, 1, :], in_=own, axis=AXIS_X, op=ALU.add)
            V.wait(V.done())
            V.do(nc.vector.reciprocal, small[:, 2, :], small[:, 1, :])
            V.wait(V.done())
            V.do(nc.vector.tensor_tensor, out=own, in0=own, in1=over(small[:, 2, :], 2, E), op=ALU.mult)
            V.wait(V.done())
            for t in range(QT):
                V.do(nc.vector.max, out=top[:, t, :], in_=score[:, t, 0:E])
            V.wait(V.done())
            V.do(nc.vector.tensor_copy, six[:, :, 0:TOPK], top[:, :, 0:TOPK])
            V.wait(V.done())
            for t in range(QT):
                V.do(nc.vector.match_replace, out=marked[:, t, :], in_to_replace=six[:, t, :],
                     in_values=score[:, t, :], imm_value=-2.0)
            V.wait(V.done(), *st["pos"])
            V.do(nc.vector.tensor_scalar, mask, marked[:, :, 0:E], -2.0, None, ALU.is_equal)
            masked = V.done()
            yield
            PE.wait(masked, *st["pos"])
            pos = bank[2][:, 0:QT * E].rearrange("p (t e) -> p t e", t=QT)
            for t in range(QT):
                PE.do(nc.tensor.matmul, pos[:, t, :], tri, mask[:, t, :], start=True, stop=False)
                for before in range(t):
                    PE.do(nc.tensor.matmul, pos[:, t, :], ones, mask[:, before, :], start=False, stop=False)
                PE.do(nc.tensor.matmul, pos[:, t, :], ones, seen, start=False, stop=True)
            counted = PE.done()
            V.wait(counted)
            V.do(nc.vector.tensor_scalar, valid, pos, float(CAP), None, ALU.is_lt)
            V.do(nc.vector.tensor_scalar, code, pos, -1.0, None, ALU.mult)
            st["pos"] = (V.done(),)
            V.wait(V.done())
            V.do(nc.vector.tensor_tensor, out=valid, in0=valid, in1=mask, op=ALU.mult)
            V.do(nc.vector.tensor_tensor, out=code, in0=code, in1=over(first, 1, QT), op=ALU.add)
            for t in range(QT):
                V.do(nc.vector.tensor_tensor, out=seen, in0=seen, in1=mask[:, t, :], op=ALU.add)
                V.wait(V.done())
            st["pos"] = (V.done(),)
            V.do(nc.vector.tensor_tensor, out=code, in0=code, in1=valid, op=ALU.mult)
            V.wait(V.done())
            for t in range(QT):
                V.do(nc.vector.max, out=best[:, t, :], in_=code[:, t, :])
            coded = V.done()
            yield
            s = q % 2
            V.wait(coded, *st["where"][s])
            V.do(nc.vector.tensor_scalar, where[s], best, -1.0, float(SLOTS), ALU.mult, ALU.add)
            for t in range(QT):
                V.do(nc.vector.tensor_tensor, out=equal[:, t * TOPK:(t + 1) * TOPK, :],
                     in0=over(code[:, t, :], 1, TOPK), in1=over(best[:, t, 0:TOPK], 2, E), op=ALU.is_equal)
            V.wait(V.done())
            for t in range(QT):
                V.do(nc.vector.tensor_tensor, out=equal[:, t * TOPK:(t + 1) * TOPK, :],
                     in0=equal[:, t * TOPK:(t + 1) * TOPK, :], in1=over(score[:, t, 0:E], 1, TOPK), op=ALU.mult)
            V.wait(V.done())
            V.do(nc.vector.tensor_reduce, out=pair[s].rearrange("p t k w -> p (t k) w")[:, :, 1], in_=equal,
                 axis=AXIS_X, op=ALU.add)
            V.do(nc.vector.tensor_copy, pair[s][:, :, :, 0], over(token[:, q * QT:(q + 1) * QT], 2, TOPK))
            st["score"] = (V.done(),)
            G.wait(V.done(), padded)
            for t in range(QT):
                for k in range(TOPK):
                    mark = G.dma(nc.gpsimd.indirect_dma_start, prog.slot(f"ff_s{s}"), out=tab[:, :],
                                 out_offset=bass.IndirectOffsetOnAxis(ap=where[s][:, t, k:k + 1], axis=0),
                                 in_=pair[s][:, t, k, :], in_offset=None, bounds_check=SLOTS - 1,
                                 oob_is_err=False)
            prog.open.append(mark)
            st["where"][s] = (mark,)
            st["table"] = st["where"][0] + st["where"][1]
            yield

        wload, up_free, down_free = {}, [()] * nw, [()] * nw

        def load_up(e):
            r = e % nw
            SP.wait(*up_free[r])
            prog.load(f"ff_w{r}", ring[r][0], d["w_gate"][e].rearrange("(p c) i -> p c i", c=HC))
            wload[e, "up"] = prog.load(f"ff_w{r}", ring[r][1], d["w_up"][e].rearrange("(p c) i -> p c i", c=HC))

        def load_down(e):
            r = e % nw
            dn = ring[r][2]
            SP.wait(*down_free[r])
            prog.load(f"ff_d{r}", dn[:, 0:2, :], d["w_down"][e, 0:2 * P, :].rearrange("(j p) h -> p j h", p=P))
            wload[e, "down"] = prog.load(f"ff_d{r}", dn[0:last, 2, :], d["w_down"][e, 2 * P:, :])

        coming = iter(())
        fronts = range(fronted, NQ)
        if fronted == 0:
            fronts = fronts[1:]
            for _ in turn_quad(0):
                pass
        for q in range(NQ):
            if q < len(fronts):
                coming = turn_quad(fronts[q])
            for step, _ in enumerate(route(q)):
                if step in front_at:
                    next(coming, None)
                self.spend(early[step])
            for _ in coming:
                pass
            if q == 1:
                for e in range(AHEAD):
                    load_up(e)
                    load_down(e)
        V.do(nc.vector.memset, bank[3][last:P, :], 0.0)
        routed = (V.done(), PE.done(), A.done(), G.done()) + self.xn_free
        SP.wait(*st["table"])
        prog.load("ff_tab", tab2, tab.rearrange("(q c) t -> c q t", c=PAIR))
        read = prog.load("ff_tab", tab1[0:CAP], tab.rearrange("(e c) t -> c e t", c=CAP))
        self.spend(2)
        V.wait(read)
        V.do(nc.vector.tensor_copy, ids, tab2[:, :, 0])
        V.do(nc.vector.tensor_copy, wts, tab2[:, :, 1])
        V.do(nc.vector.tensor_copy, ids1[0:CAP, :], tab1[0:CAP, :, 0])
        listed = V.done()

        sb.at = region
        ring += [weights() for _ in range(nw - AHEAD)]
        xeT = [sb.cut([HC, PAIR]) for _ in range(2)]
        sg, hid = sb.cut([INTER]), sb.cut([INTER])
        hT = [sb.cut([IC, PAIR]) for _ in range(2)]
        ye = [sb.base[:, self.start:self.start + H]] + [sb.cut([H]) for _ in range(ny - 1)]
        for lane in (SP, V, A, G, PE):
            lane.wait(*routed, listed, prog.open[pads])
        G.wait(*x_free[0], *x_free[1], *self.xn_free, prog.open[pads])
        xe_free, xeT_free, hT_free, ye_free = [()] * nx, [(), ()], [(), ()], [()] * ny
        o = {"t": (), "gu": (), "sg": (), "flip": (), "y": ()}
        xeload, turned, hidden, flipped = {}, {}, {}, {}

        def gather(p):
            s = p % nx
            G.wait(*xe_free[s])
            xeload[p] = G.dma(nc.gpsimd.indirect_dma_start, prog.slot(f"ff_xe{s}"), out=xe[s],
                              out_offset=None, in_=xn_dram[:, :],
                              in_offset=bass.IndirectOffsetOnAxis(ap=ids[:, p:p + 1], axis=0),
                              bounds_check=T + CAP - 1, oob_is_err=True)
            prog.open.append(xeload[p])

        def turn(p):
            PE.wait(xeload[p], *o["t"])
            cols = xe[p % nx].rearrange("p (m c) -> p c m", c=HC)
            for c in range(HC):
                PE.do(nc.tensor.transpose, bank[0][:, c * PAIR:(c + 1) * PAIR], cols[:, c, :], prog.ident)
            xe_free[p % nx] = (PE.done(),)
            V.wait(PE.done(), *xeT_free[p % 2])
            V.do(nc.vector.tensor_copy, xeT[p % 2], bank[0][:, :].rearrange("p (c t) -> p c t", c=HC))
            turned[p] = V.done()
            o["t"] = (V.done(),)

        def up(p):
            PE.wait(wload[2 * p, "up"], wload[2 * p + 1, "up"], turned[p], *o["gu"])
            for w in range(2):
                for c in range(HC):
                    for half in range(2):
                        mine = slice(half * CAP, (half + 1) * CAP)
                        PE.do(nc.tensor.matmul, bank[1 + w][mine, 0:INTER], xeT[p % 2][:, c, mine],
                              ring[(2 * p + half) % nw][w][:, c, :], start=c == 0, stop=c == HC - 1)
                if w == 0:
                    A.wait(PE.done(), *o["sg"])
                    A.do(nc.scalar.activation, sg, bank[1][:, 0:INTER], ACT.Silu)
            xeT_free[p % 2] = (PE.done(),)
            for e in (2 * p, 2 * p + 1):
                up_free[e % nw] = (PE.done(),)
                if e + nw < E:
                    load_up(e + nw)
            V.wait(A.done(), PE.done(), *o["flip"])
            V.do(nc.vector.tensor_tensor, out=hid, in0=sg, in1=bank[2][:, 0:INTER], op=ALU.mult)
            o["gu"] = o["sg"] = (V.done(),)
            hidden[p] = V.done()

        def flip(p):
            PE.wait(hidden[p], *o.get("flipped", ()))
            for j in range(IC):
                m = P if j < 2 else last
                PE.do(nc.tensor.transpose, bank[3][0:m, j * PAIR:(j + 1) * PAIR], hid[:, j * P:j * P + m],
                      prog.ident)
            o["flip"] = (PE.done(),)
            A.wait(PE.done(), *hT_free[p % 2])
            A.do(nc.scalar.copy, hT[p % 2], bank[3][:, 0:IC * PAIR].rearrange("p (j t) -> p j t", j=IC))
            flipped[p] = A.done()
            o["flipped"] = (A.done(),)

        def down(p):
            s = p % 2
            PE.wait(flipped[p], wload[2 * p, "down"], wload[2 * p + 1, "down"], *o["y"])
            for j in range(IC):
                m = P if j < 2 else last
                for half in range(2):
                    mine = slice(half * CAP, (half + 1) * CAP)
                    PE.do(nc.tensor.matmul, bank[4][mine, :], hT[s][0:m, j, mine],
                          ring[(2 * p + half) % nw][2][0:m, j, :], start=j == 0, stop=j == IC - 1)
            hT_free[s] = (PE.done(),)
            for half in range(2):
                e = 2 * p + half
                down_free[e % nw] = (PE.done(),)
                if e + nw < E:
                    load_down(e + nw)
            o["sums"] = [(0, PE.done()), (1, PE.done())]

        def add_expert(p):
            half, made = o["sums"].pop(0)
            mine = slice(half * CAP, (half + 1) * CAP)
            e = 2 * p + half
            A.wait(made, *ye_free[e % ny])
            A.do(nc.scalar.activation, ye[e % ny][0:CAP, :], bank[4][mine, :], ACT.Copy, scale=wts[mine, p:p + 1])
            o["y"] = (A.done(),)
            G.wait(A.done())
            ye_free[e % ny] = (self.add_rows(ye[e % ny][0:CAP, :], ids1[0:CAP, e:e + 1]),)

        self.spend(2)
        self.take_products()
        assert len(self.units) <= (NQ - self.direct) * (self.SC + QT)
        self.queue_sums()
        G.wait(*(mark for marks in self.so_free for mark in marks))
        for n in range(nx):
            gather(n)
        for e in range(AHEAD, nw):
            load_up(e)
            load_down(e)
        turn(0)
        gather(nx)
        left = len(self.units)
        for p in range(NPAIR + 1):
            if p < NPAIR:
                up(p)
            if p > 0:
                down(p - 1)
                add_expert(p - 1)
            if p < NPAIR:
                flip(p)
                if p + 1 < NPAIR:
                    turn(p + 1)
                self.spend(len(self.units) - left * (NPAIR - 1 - p) // NPAIR)
                if p + 1 + nx < NPAIR:
                    gather(p + 1 + nx)
            if p > 0:
                add_expert(p - 1)
        self.take_products()
        self.queue_sums()
        prog.stage_end()
        sb.at = self.start


def build(nc, dram, stages="SAF"):
    with ExitStack() as ctx:
        p = Program(nc, ctx, dram)
        p.constants()
        if "S" in stages:
            ff = FeedForward(p, dram["x1"], dram["y"], (6, 7, 6), DIRECT[0], BATCH)
            turned = [p.sb.cut([HC, BANK]) for _ in range(2)]
            for q in range(BESIDE_SCAN):
                ff.xnT[q] = turned[q % 2]
            p.state_space(dram["x"], dram["x1"], ff, BESIDE_SCAN)
            ff.take_banks(5, 6, 7)
            for q in range(BESIDE_SCAN, BATCH):
                ff.xnT[q] = p.sb.cut([HC, BANK])
            ff.rest(BESIDE_SCAN, UNITS[0], FRONT_AT[0], 5, 3, 4)
        if "A" in stages:
            p.attention(dram["y"], dram["x3"])
        if "F" in stages:
            ff = FeedForward(p, dram["x3"], dram["out"], (5, 6, 7), DIRECT[1], 2)
            ff.keep_all()
            ff.rest(0, UNITS[1], FRONT_AT[1], 4, 2, 2)
        block = ctx.enter_context(nc.Block())
        PE, V, A, G, SP = p.lanes

        @block.tensor
        def _(eng):
            PE.play(eng)

        @block.vector
        def _(eng):
            V.play(eng)

        @block.scalar
        def _(eng):
            A.play(eng)

        @block.gpsimd
        def _(eng):
            G.play(eng)

        @block.sync
        def _(eng):
            SP.play(eng)


def rope_factor():
    f = np.float32
    inv = f(10000.0) ** (f(-2.0) * np.arange(HEAD // 2, dtype=f) / f(HEAD))
    theta = np.arange(SEQ, dtype=f)[:, None] * inv[None, :]
    both = (np.cos(theta) + np.sin(theta)).astype(f)
    return np.ascontiguousarray(np.tile(np.concatenate([both, both], axis=1).T, (P // HEAD, 1)))


def lay_out(inputs):
    g = {k: np.asarray(v) for k, v in inputs.items()}
    heads = np.arange(HEADS * HEAD).reshape(4, 4, HEAD).transpose(1, 0, 2).ravel()
    c = np.ascontiguousarray
    return {
        "x": c(g["L0_attn_a_x"].reshape(T, H)),
        "wxT": c(g["L0_attn_a_W_x"].T), "wdtT": c(g["L0_attn_a_W_dt"].T),
        "par": c(np.stack([g["L0_attn_a_b_dt"], g["L0_attn_a_D_param"]], 1).reshape(HC, P, 2).transpose(1, 0, 2)),
        "A_log": c(g["L0_attn_a_A_log"]),
        "wqT": c(g["L0_attn_b_Wq"][heads].T), "bq": c(g["L0_attn_b_bq"][heads].reshape(HC, P).T),
        "wkT": c(g["L0_attn_b_Wk"].T), "bk": c(g["L0_attn_b_bk"].reshape(P, 1)),
        "wvT": c(g["L0_attn_b_Wv"].T), "bv": c(g["L0_attn_b_bv"]),
        "woT": c(g["L0_attn_b_Wo"].T[heads]), "bo": c(g["L0_attn_b_bo"]),
        "gate_wT": c(g["L0_ffn_gate_w"].T),
        "w_gate": c(g["L0_ffn_w_gate"]), "w_up": c(g["L0_ffn_w_up"]), "w_down": c(g["L0_ffn_w_down"]),
        "sw_gate": c(g["L0_ffn_sw_gate"]), "sw_up": c(g["L0_ffn_sw_up"]), "sw_down": c(g["L0_ffn_sw_down"]),
        "rope": rope_factor(),
    }


SCRATCH = {"bc": (BATCH, 2 * NSTATE, SEQ), "x1": (T, H), "x3": (T, H),
           "y": (T + CAP, H), "xn": (T + CAP, H), "tab": (SLOTS, 2)}


def declare(nc, arrays, stages="SAF"):
    dram = {n: nc.dram_tensor(f"in_{n}", a.shape, FP32, kind="ExternalInput").ap() for n, a in arrays.items()}
    for n, shape in SCRATCH.items():
        if n not in dram:
            dram[n] = nc.dram_tensor(f"scratch_{n}", shape, FP32).ap()
    dram["out"] = nc.dram_tensor("out", (T + CAP, H), FP32, kind="ExternalOutput").ap()
    build(nc, dram, stages)


def kernel(**inputs):
    import concourse.bacc as bacc
    from concourse.bass_utils import run_bass_kernel_spmd

    arrays = lay_out(inputs)
    nc = bacc.Bacc("TRN2", target_bir_lowering=False, num_devices=1)
    declare(nc, arrays)
    r = run_bass_kernel_spmd(nc, [{f"in_{n}": a for n, a in arrays.items()}], core_ids=[0])
    return r.results[0]["out"][0:T].reshape(BATCH, SEQ, H)
```
